# Optimizing a Trainium2 kernel written in Bass

```python
import numpy as np
import jax
import jax.numpy as jnp

def _softmax(x, axis=-1):
    return jax.nn.softmax(x, axis=axis)

def _gelu(x):
    return jax.nn.gelu(x, approximate=True)

def _silu(x):
    return jax.nn.silu(x)

def _sigmoid(x):
    return jax.nn.sigmoid(x)

def _layernorm(x, axis=-1, eps=1e-05):
    m = jnp.mean(x, axis=axis, keepdims=True)
    v = jnp.var(x, axis=axis, keepdims=True)
    return (x - m) / jnp.sqrt(v + eps)

def _scatter_add(tgt, idx, src, axis=0):
    return tgt.at[idx].add(src)

def _segment_sum(src, seg, n):
    return jax.ops.segment_sum(src, seg, n)
kernel_name = 'mk_dlrm_tower_d1_rec_r8_af9abd'

def setup_inputs(seed: int=0):
    np.random.seed(seed)
    _w = jnp.asarray

    def _rec_inputs():
        import jax
        import jax.numpy as jnp
        _tk = jax.random.key(seed)
        dense_ctx = jax.random.normal(jax.random.fold_in(_tk, 190), (512, 16), jnp.float32)
        ids = jnp.stack([jax.random.randint(jax.random.fold_in(_tk, 200 + f), (512,), 0, v, jnp.int32) for f, v in enumerate([125000, 1000, 1250, 12500, 1250, 1000, 125000, 1250, 1000, 1000, 1000, 12500, 125000, 12500, 1250, 125000, 12500, 1250, 1250, 125000, 1250, 1250, 12500, 1000, 12500, 125000, 1250, 125000, 12500, 125000, 125000, 1250, 1000, 125000, 1000, 125000, 12500, 1250, 12500])], axis=1)
        tbl_0 = 0.05 * jax.random.normal(jax.random.fold_in(_tk, 500 + 0), (125000, 16), jnp.float32)
        tbl_1 = 0.05 * jax.random.normal(jax.random.fold_in(_tk, 500 + 1), (1000, 16), jnp.float32)
        tbl_2 = 0.05 * jax.random.normal(jax.random.fold_in(_tk, 500 + 2), (1250, 16), jnp.float32)
        tbl_3 = 0.05 * jax.random.normal(jax.random.fold_in(_tk, 500 + 3), (12500, 16), jnp.float32)
        tbl_4 = 0.05 * jax.random.normal(jax.random.fold_in(_tk, 500 + 4), (1250, 16), jnp.float32)
        tbl_5 = 0.05 * jax.random.normal(jax.random.fold_in(_tk, 500 + 5), (1000, 16), jnp.float32)
        tbl_6 = 0.05 * jax.random.normal(jax.random.fold_in(_tk, 500 + 6), (125000, 16), jnp.float32)
        tbl_7 = 0.05 * jax.random.normal(jax.random.fold_in(_tk, 500 + 7), (1250, 16), jnp.float32)
        tbl_8 = 0.05 * jax.random.normal(jax.random.fold_in(_tk, 500 + 8), (1000, 16), jnp.float32)
        tbl_9 = 0.05 * jax.random.normal(jax.random.fold_in(_tk, 500 + 9), (1000, 16), jnp.float32)
        tbl_10 = 0.05 * jax.random.normal(jax.random.fold_in(_tk, 500 + 10), (1000, 16), jnp.float32)
        tbl_11 = 0.05 * jax.random.normal(jax.random.fold_in(_tk, 500 + 11), (12500, 16), jnp.float32)
        tbl_12 = 0.05 * jax.random.normal(jax.random.fold_in(_tk, 500 + 12), (125000, 16), jnp.float32)
        tbl_13 = 0.05 * jax.random.normal(jax.random.fold_in(_tk, 500 + 13), (12500, 16), jnp.float32)
        tbl_14 = 0.05 * jax.random.normal(jax.random.fold_in(_tk, 500 + 14), (1250, 16), jnp.float32)
        tbl_15 = 0.05 * jax.random.normal(jax.random.fold_in(_tk, 500 + 15), (125000, 16), jnp.float32)
        tbl_16 = 0.05 * jax.random.normal(jax.random.fold_in(_tk, 500 + 16), (12500, 16), jnp.float32)
        tbl_17 = 0.05 * jax.random.normal(jax.random.fold_in(_tk, 500 + 17), (1250, 16), jnp.float32)
        tbl_18 = 0.05 * jax.random.normal(jax.random.fold_in(_tk, 500 + 18), (1250, 16), jnp.float32)
        tbl_19 = 0.05 * jax.random.normal(jax.random.fold_in(_tk, 500 + 19), (125000, 16), jnp.float32)
        tbl_20 = 0.05 * jax.random.normal(jax.random.fold_in(_tk, 500 + 20), (1250, 16), jnp.float32)
        tbl_21 = 0.05 * jax.random.normal(jax.random.fold_in(_tk, 500 + 21), (1250, 16), jnp.float32)
        tbl_22 = 0.05 * jax.random.normal(jax.random.fold_in(_tk, 500 + 22), (12500, 16), jnp.float32)
        tbl_23 = 0.05 * jax.random.normal(jax.random.fold_in(_tk, 500 + 23), (1000, 16), jnp.float32)
        tbl_24 = 0.05 * jax.random.normal(jax.random.fold_in(_tk, 500 + 24), (12500, 16), jnp.float32)
        tbl_25 = 0.05 * jax.random.normal(jax.random.fold_in(_tk, 500 + 25), (125000, 16), jnp.float32)
        tbl_26 = 0.05 * jax.random.normal(jax.random.fold_in(_tk, 500 + 26), (1250, 16), jnp.float32)
        tbl_27 = 0.05 * jax.random.normal(jax.random.fold_in(_tk, 500 + 27), (125000, 16), jnp.float32)
        tbl_28 = 0.05 * jax.random.normal(jax.random.fold_in(_tk, 500 + 28), (12500, 16), jnp.float32)
        tbl_29 = 0.05 * jax.random.normal(jax.random.fold_in(_tk, 500 + 29), (125000, 16), jnp.float32)
        tbl_30 = 0.05 * jax.random.normal(jax.random.fold_in(_tk, 500 + 30), (125000, 16), jnp.float32)
        tbl_31 = 0.05 * jax.random.normal(jax.random.fold_in(_tk, 500 + 31), (1250, 16), jnp.float32)
        tbl_32 = 0.05 * jax.random.normal(jax.random.fold_in(_tk, 500 + 32), (1000, 16), jnp.float32)
        tbl_33 = 0.05 * jax.random.normal(jax.random.fold_in(_tk, 500 + 33), (125000, 16), jnp.float32)
        tbl_34 = 0.05 * jax.random.normal(jax.random.fold_in(_tk, 500 + 34), (1000, 16), jnp.float32)
        tbl_35 = 0.05 * jax.random.normal(jax.random.fold_in(_tk, 500 + 35), (125000, 16), jnp.float32)
        tbl_36 = 0.05 * jax.random.normal(jax.random.fold_in(_tk, 500 + 36), (12500, 16), jnp.float32)
        tbl_37 = 0.05 * jax.random.normal(jax.random.fold_in(_tk, 500 + 37), (1250, 16), jnp.float32)
        tbl_38 = 0.05 * jax.random.normal(jax.random.fold_in(_tk, 500 + 38), (12500, 16), jnp.float32)
        _rk = jax.random.fold_in(_tk, 7)
        W_top1 = 0.0606339 * jax.random.normal(jax.random.fold_in(_tk, 801), (272, 512), jnp.float32)
        W_top2 = 0.0441942 * jax.random.normal(jax.random.fold_in(_tk, 802), (512, 256), jnp.float32)
        W_top3 = 0.0625 * jax.random.normal(jax.random.fold_in(_tk, 803), (256, 1), jnp.float32)
        b_top1 = jnp.zeros((512,), jnp.float32)
        b_top2 = jnp.zeros((256,), jnp.float32)
        return (dense_ctx, ids, tbl_0, tbl_1, tbl_2, tbl_3, tbl_4, tbl_5, tbl_6, tbl_7, tbl_8, tbl_9, tbl_10, tbl_11, tbl_12, tbl_13, tbl_14, tbl_15, tbl_16, tbl_17, tbl_18, tbl_19, tbl_20, tbl_21, tbl_22, tbl_23, tbl_24, tbl_25, tbl_26, tbl_27, tbl_28, tbl_29, tbl_30, tbl_31, tbl_32, tbl_33, tbl_34, tbl_35, tbl_36, tbl_37, tbl_38, W_top1, b_top1, W_top2, b_top2, W_top3)
    dense_ctx, ids, tbl_0, tbl_1, tbl_2, tbl_3, tbl_4, tbl_5, tbl_6, tbl_7, tbl_8, tbl_9, tbl_10, tbl_11, tbl_12, tbl_13, tbl_14, tbl_15, tbl_16, tbl_17, tbl_18, tbl_19, tbl_20, tbl_21, tbl_22, tbl_23, tbl_24, tbl_25, tbl_26, tbl_27, tbl_28, tbl_29, tbl_30, tbl_31, tbl_32, tbl_33, tbl_34, tbl_35, tbl_36, tbl_37, tbl_38, W_top1, b_top1, W_top2, b_top2, W_top3 = _rec_inputs()

    def _L0_rec_setup():
        import jax, jax.numpy as jnp
        import numpy as np
        B, M0, D = (256, 39, 16)
        CIN_SIZE = [128, 128]

        def _cin(inputs, weights):
            X0 = inputs
            Xi = inputs
            res = []
            for W in weights:
                mi = Xi.shape[1]
                z = jnp.einsum('bmd,bnd->bdmn', X0, Xi)
                z = z.reshape(z.shape[0], z.shape[1], M0 * mi)
                Xi = jnp.einsum('bdp,po->bod', z, W)
                res.append(Xi)
            res = jnp.concatenate(res, axis=1)
            return jnp.sum(res, axis=-1)
        key = jax.random.key(seed)
        k1, k2, k3 = jax.random.split(key, 3)
        inputs = jax.random.normal(k1, (B, M0, D), dtype=jnp.float32)
        W0 = jax.random.normal(k2, (M0 * M0, CIN_SIZE[0]), dtype=jnp.float32) * 0.05
        W1 = jax.random.normal(k3, (M0 * CIN_SIZE[0], CIN_SIZE[1]), dtype=jnp.float32) * 0.05
        return {'inputs': inputs, 'W0': W0, 'W1': W1}
    _L0_rec_all = _L0_rec_setup()
    _L0_rec_in = {k: v for k, v in _L0_rec_all.items() if k in ('W0', 'W1')}
    del _L0_rec_all
    return {'dense_ctx': dense_ctx, 'ids': ids, 'tbl_0': tbl_0, 'tbl_1': tbl_1, 'tbl_2': tbl_2, 'tbl_3': tbl_3, 'tbl_4': tbl_4, 'tbl_5': tbl_5, 'tbl_6': tbl_6, 'tbl_7': tbl_7, 'tbl_8': tbl_8, 'tbl_9': tbl_9, 'tbl_10': tbl_10, 'tbl_11': tbl_11, 'tbl_12': tbl_12, 'tbl_13': tbl_13, 'tbl_14': tbl_14, 'tbl_15': tbl_15, 'tbl_16': tbl_16, 'tbl_17': tbl_17, 'tbl_18': tbl_18, 'tbl_19': tbl_19, 'tbl_20': tbl_20, 'tbl_21': tbl_21, 'tbl_22': tbl_22, 'tbl_23': tbl_23, 'tbl_24': tbl_24, 'tbl_25': tbl_25, 'tbl_26': tbl_26, 'tbl_27': tbl_27, 'tbl_28': tbl_28, 'tbl_29': tbl_29, 'tbl_30': tbl_30, 'tbl_31': tbl_31, 'tbl_32': tbl_32, 'tbl_33': tbl_33, 'tbl_34': tbl_34, 'tbl_35': tbl_35, 'tbl_36': tbl_36, 'tbl_37': tbl_37, 'tbl_38': tbl_38, 'W_top1': W_top1, 'b_top1': b_top1, 'W_top2': W_top2, 'b_top2': b_top2, 'W_top3': W_top3, 'L0_rec_W0': _L0_rec_in['W0'], 'L0_rec_W1': _L0_rec_in['W1']}

def reference(dense_ctx, ids, tbl_0, tbl_1, tbl_2, tbl_3, tbl_4, tbl_5, tbl_6, tbl_7, tbl_8, tbl_9, tbl_10, tbl_11, tbl_12, tbl_13, tbl_14, tbl_15, tbl_16, tbl_17, tbl_18, tbl_19, tbl_20, tbl_21, tbl_22, tbl_23, tbl_24, tbl_25, tbl_26, tbl_27, tbl_28, tbl_29, tbl_30, tbl_31, tbl_32, tbl_33, tbl_34, tbl_35, tbl_36, tbl_37, tbl_38, W_top1, b_top1, W_top2, b_top2, W_top3, L0_rec_W0, L0_rec_W1):
    import jax
    import jax.numpy as jnp

    def _L0_rec_ref(inputs, W0, W1):
        import jax, jax.numpy as jnp
        import numpy as np
        B, M0, D = (256, 39, 16)
        CIN_SIZE = [128, 128]

        def _cin(inputs, weights):
            X0 = inputs
            Xi = inputs
            res = []
            for W in weights:
                mi = Xi.shape[1]
                z = jnp.einsum('bmd,bnd->bdmn', X0, Xi)
                z = z.reshape(z.shape[0], z.shape[1], M0 * mi)
                Xi = jnp.einsum('bdp,po->bod', z, W)
                res.append(Xi)
            res = jnp.concatenate(res, axis=1)
            return jnp.sum(res, axis=-1)
        return _cin(inputs, [W0, W1])
    e = jnp.stack([tbl_0[ids[:, 0]], tbl_1[ids[:, 1]], tbl_2[ids[:, 2]], tbl_3[ids[:, 3]], tbl_4[ids[:, 4]], tbl_5[ids[:, 5]], tbl_6[ids[:, 6]], tbl_7[ids[:, 7]], tbl_8[ids[:, 8]], tbl_9[ids[:, 9]], tbl_10[ids[:, 10]], tbl_11[ids[:, 11]], tbl_12[ids[:, 12]], tbl_13[ids[:, 13]], tbl_14[ids[:, 14]], tbl_15[ids[:, 15]], tbl_16[ids[:, 16]], tbl_17[ids[:, 17]], tbl_18[ids[:, 18]], tbl_19[ids[:, 19]], tbl_20[ids[:, 20]], tbl_21[ids[:, 21]], tbl_22[ids[:, 22]], tbl_23[ids[:, 23]], tbl_24[ids[:, 24]], tbl_25[ids[:, 25]], tbl_26[ids[:, 26]], tbl_27[ids[:, 27]], tbl_28[ids[:, 28]], tbl_29[ids[:, 29]], tbl_30[ids[:, 30]], tbl_31[ids[:, 31]], tbl_32[ids[:, 32]], tbl_33[ids[:, 33]], tbl_34[ids[:, 34]], tbl_35[ids[:, 35]], tbl_36[ids[:, 36]], tbl_37[ids[:, 37]], tbl_38[ids[:, 38]]], axis=1)
    z = _L0_rec_ref(e, L0_rec_W0, L0_rec_W1)
    z = z.reshape(z.shape[0], -1)
    h = jnp.concatenate([z, dense_ctx], axis=1)
    h = jnp.maximum(h @ W_top1 + b_top1, 0.0)
    h = jnp.maximum(h @ W_top2 + b_top2, 0.0)
    y = h @ W_top3
    return y

_drawn_inputs = setup_inputs


def setup_inputs(seed=0):
    import zlib

    import numpy as np

    out = dict(_drawn_inputs(seed))
    spreads = {'b_top1': (0.0, 0.1), 'b_top2': (0.0, 0.1)}
    factors = {'tbl_0': 4.9,
     'tbl_1': 5.508,
     'tbl_2': 4.817,
     'tbl_3': 5.348,
     'tbl_4': 5.027,
     'tbl_5': 5.236,
     'tbl_6': 4.787,
     'tbl_7': 4.918,
     'tbl_8': 5.182,
     'tbl_9': 4.957,
     'tbl_10': 5.194,
     'tbl_11': 5.165,
     'tbl_12': 4.914,
     'tbl_13': 4.776,
     'tbl_14': 4.804,
     'tbl_15': 5.017,
     'tbl_16': 5.134,
     'tbl_17': 5.082,
     'tbl_18': 5.493,
     'tbl_19': 4.99,
     'tbl_20': 5.172,
     'tbl_21': 5.072,
     'tbl_22': 4.901,
     'tbl_23': 5.013,
     'tbl_24': 4.666,
     'tbl_25': 4.574,
     'tbl_26': 5.014,
     'tbl_27': 5.602,
     'tbl_28': 4.717,
     'tbl_29': 5.041,
     'tbl_30': 5.289,
     'tbl_31': 4.656,
     'tbl_32': 5.084,
     'tbl_33': 5.211,
     'tbl_34': 5.181,
     'tbl_35': 5.153,
     'tbl_36': 4.887,
     'tbl_37': 4.9,
     'tbl_38': 5.241,
     'L0_rec_W1': 5.421}
    for name, (base, spread) in spreads.items():
        noise = np.random.default_rng([zlib.crc32(name.encode()), seed]).standard_normal(out[name].shape)
        drawn = base * np.exp(spread * noise) if base else spread * noise
        out[name] = jnp.asarray(drawn.astype(out[name].dtype))
    for name, factor in factors.items():
        out[name] = (out[name] * factor).astype(out[name].dtype)
    return out
```

```python
from contextlib import ExitStack

import concourse.bass as bass
import concourse.mybir as mybir
import numpy as np

F = 39
D = 16
B = 512
O = 128
P = 128
TILES = B // P
SHIFTS = (F + 1) // 2
PER = 3
R = PER * F
PT = -(-SHIFTS // PER)
ROWS = [min(PER, SHIFTS - PER * t) * F for t in range(PT)]
CH = 512
CB = CH // D
CPT = P // CB
CHUNKS = TILES * CPT
SUBS = CH // P
SB = P // D
GW = F + 1
UPC = -(-PT // 2)
UNITS = CHUNKS * UPC
UPT = CPT * UPC
LAG = 2
GOFF = UPC + LAG + 1
GROUPS = [(0, 13), (13, 26), (26, F)]
SPLIT_AT = [4, 9, 12]
X_AT = UPT - 2
S2_STEPS = 12
HID1, HID2, DC = 512, 256, 16
H1T, H2T = HID1 // P, HID2 // P
XJ = 2
PREP = XJ + 2 * CPT


def unit_tiles(p):
    return [t for t in (2 * p, 2 * p + 1) if t < PT]


def build(nc, ids, tables, dense_t, w0_pair, w0_mirror, w1, wt1, bt1, wt2, bt2, wt3, select, ident16, ident32, out):
    f32, bf16, f32r, i32 = mybir.dt.float32, mybir.dt.bfloat16, mybir.dt.float32r, mybir.dt.int32
    ACT, ALU = mybir.ActivationFunctionType, mybir.AluOpType
    ctx = ExitStack()
    with ctx:
        def sb(name, shape, dt=f32):
            return ctx.enter_context(nc.sbuf_tensor(name, shape, dt))

        def bank(name):
            return ctx.enter_context(nc.psum_tensor(name, [P, 512], f32))

        def sem(name):
            return ctx.enter_context(nc.semaphore(name))

        ids_sb = sb("ids_sb", [P, TILES, F], i32)
        emb = sb("emb", [P, TILES, F * D])
        parts = sb("parts", [P, 3, F * D], bf16)
        xs = sb("xs", [R, 2, P, D], bf16)
        xa = sb("xa", [R, 2, P, D])
        sel = sb("sel", [R, PT + 1, R], bf16)
        id16 = sb("id16", [P, P], bf16)
        id32 = sb("id32", [P, P])
        z = sb("z", [R, 2, 2, CH])
        z_hi = sb("z_hi", [R, 3, 2, CH], f32r)
        z_lo = sb("z_lo", [R, 3, 2, CH], f32r)
        w0p = sb("w0p", [R, PT, O])
        w0m = sb("w0m", [R, PT, O])
        w0_hi = sb("w0_hi", [R, PT, O], f32r)
        w0_lo = sb("w0_lo", [R, PT, O], f32r)
        xi = sb("xi", [O, CH])
        xit_hi = sb("xit_hi", [P, 2, CH], f32r)
        xit_lo = sb("xit_lo", [P, 2, CH], f32r)
        xt = sb("xt", [P, 2, 2, SUBS, GW], f32r)
        diag = sb("diag", [P, 2, 2, SUBS, SB, GW], f32r)
        g = sb("g", [O, 2, GW, P])
        w1_sb = sb("w1_sb", [O, F, O])
        z1 = sb("z1", [O, B])
        z2 = sb("z2", [O, B])
        dt_sb = sb("dt_sb", [DC, B])
        wt1_sb = sb("wt1_sb", [P, 2, HID1])
        wt1c_sb = sb("wt1c_sb", [DC, HID1])
        wt2_sb = sb("wt2_sb", [P, H1T, HID2])
        wt3_sb = sb("wt3_sb", [P, H2T])
        bt1_sb = sb("bt1_sb", [P, H1T])
        bt2_sb = sb("bt2_sb", [P, H2T])
        hidden = g[:, 0, :, :].rearrange("p m b -> p (m b)")
        h1 = hidden[:, 0:H1T * B].rearrange("p (k b) -> p k b", b=B)
        h2 = hidden[:, H1T * B:(H1T + H2T) * B].rearrange("p (k b) -> p k b", b=B)
        y_sb = sb("y_sb", [1, B])

        b_bank = [bank(f"b_bank{j}") for j in range(3)]
        l1_bank = bank("l1_bank")
        xit_bank = bank("xit_bank")
        prep_bank = bank("prep_bank")
        g_bank = bank("g_bank")
        s2_bank = bank("s2_bank")
        prep16 = prep_bank[:, :].bitcast(bf16)

        ids_in = sem("ids_in")
        consts_in = sem("consts_in")
        w0_in = sem("w0_in")
        w1_in = sem("w1_in")
        mlp_in = sem("mlp_in")
        gathered = [[sem(f"gathered{bt}_{k}") for k in range(len(GROUPS))] for bt in range(TILES)]
        hi_cast = sem("hi_cast")
        rest1 = sem("rest1")
        mid_cast = sem("mid_cast")
        lo_cast = sem("lo_cast")
        prep_filled = sem("prep_filled")
        prep_taken = sem("prep_taken")
        xt_hi_done = sem("xt_hi_done")
        w0_summed = sem("w0_summed")
        w0_split = sem("w0_split")
        zeroed = sem("zeroed")
        selected = sem("selected")
        product = sem("product")
        rounded = sem("rounded")
        remainder = sem("remainder")
        l1_used = sem("l1_used")
        xi_copied = sem("xi_copied")
        xi_turned = sem("xi_turned")
        xit_hi_done = sem("xit_hi_done")
        xit_lo_done = sem("xit_lo_done")
        diag_in = [sem(f"diag_in{j}") for j in range(2)]
        g_summed = sem("g_summed")
        g_copied = sem("g_copied")
        s2_done = sem("s2_done")
        z_copied = sem("z_copied")
        mlp_mm = sem("mlp_mm")
        mlp_act = sem("mlp_act")
        y_copied = sem("y_copied")
        y_out = sem("y_out")

        block = ctx.enter_context(nc.Block())

        def x_job(bt, k):
            return PREP * bt + k

        def a_job(bt, c):
            return PREP * bt + XJ + 2 * c

        def xt_job(bt, c):
            return PREP * bt + XJ + 1 + 2 * c

        def q_of(u, j=0):
            return u // UPC * PT + 2 * (u % UPC) + j

        GATE = [0, 3 * P, B]
        MLP_MM = H1T + H2T + 1

        @block.gpsimd
        def _(pool):
            pool.wait_ge(ids_in, 16)
            for bt in range(TILES):
                for k, (lo, hi) in enumerate(GROUPS):
                    for f in range(lo, hi):
                        nc.gpsimd.indirect_dma_start(
                            emb[:, bt, f * D:(f + 1) * D], None, tables[f],
                            bass.IndirectOffsetOnAxis(ids_sb[:, bt, f:f + 1], 0)).then_inc(gathered[bt][k], 16)

        @block.sync
        def _(sp):
            sp.dma_start(ids_sb[:], ids).then_inc(ids_in, 16)
            sp.dma_start(w0p[:], w0_pair.rearrange("t p o -> p t o")).then_inc(w0_in, 16)
            sp.dma_start(w0m[:], w0_mirror.rearrange("t p o -> p t o")).then_inc(w0_in, 16)
            sp.dma_start(sel[:], select).then_inc(consts_in, 16)
            sp.dma_start(id16[:], ident16).then_inc(consts_in, 16)
            sp.dma_start(id32[:], ident32).then_inc(consts_in, 16)
            sp.dma_start(w1_sb[:], w1.rearrange("(m n) o -> n m o", n=O)).then_inc(w1_in, 16)
            sp.dma_start(wt1_sb[:], wt1[0:2 * P, :].rearrange("(k p) h -> p k h", p=P)).then_inc(mlp_in, 16)
            sp.dma_start(wt1c_sb[:], wt1[2 * P:2 * P + DC, :]).then_inc(mlp_in, 16)
            sp.dma_start(wt2_sb[:], wt2.rearrange("(k p) h -> p k h", p=P)).then_inc(mlp_in, 16)
            sp.dma_start(wt3_sb[:], wt3).then_inc(mlp_in, 16)
            sp.dma_start(bt1_sb[:], bt1).then_inc(mlp_in, 16)
            sp.dma_start(bt2_sb[:], bt2).then_inc(mlp_in, 16)
            sp.dma_start(dt_sb[:], dense_t).then_inc(mlp_in, 16)
            sp.wait_ge(zeroed, 3)
            for i in range(CHUNKS):
                sp.wait_ge(prep_taken, xt_job(i // CPT, i % CPT) + 1)
                if i >= 2:
                    sp.wait_ge(g_summed, SUBS * (i - 1))
                for b in range(SB):
                    sp.dma_start(diag[b * D:(b + 1) * D, i % 2, :, :, b, :].bitcast(f32),
                                 xt[b * D:(b + 1) * D, i % 2, :, :, :].bitcast(f32)).then_inc(diag_in[i % 2], 16)
            sp.wait_ge(y_copied, 2)
            sp.dma_start(out.rearrange("b o -> o b"), y_sb[:]).then_inc(y_out, 16)
            sp.wait_ge(y_out, 16)

        @block.scalar
        def _(act):
            def cast_hi(bt, k):
                lo, hi = (x * D for x in GROUPS[k])
                act.wait_ge(gathered[bt][k], 16 * (GROUPS[k][1] - GROUPS[k][0]))
                if bt:
                    act.wait_ge(prep_filled, x_job(bt - 1, XJ - 1) + 1)
                nc.scalar.activation(parts[:, 0, lo:hi], emb[:, bt, lo:hi], ACT.Copy).then_inc(hi_cast, 1)

            def cast_mid(bt, k):
                lo, hi = (x * D for x in GROUPS[k])
                act.wait_ge(rest1, len(GROUPS) * bt + k + 1)
                nc.scalar.activation(parts[:, 1, lo:hi], emb[:, bt, lo:hi], ACT.Copy).then_inc(mid_cast, 1)

            def take_x(bt, k):
                act.wait_ge(prep_filled, x_job(bt, k) + 1)
                nc.scalar.activation(
                    xs[:, bt % 2, :, k * D // XJ:(k + 1) * D // XJ],
                    prep16[0:R, :].rearrange("p (d b) -> p b d", b=P),
                    ACT.Copy).then_inc(prep_taken, 1)

            def take_a(bt, c):
                act.wait_ge(prep_filled, a_job(bt, c) + 1)
                nc.scalar.activation(xa[:, bt % 2, c * CB:(c + 1) * CB, :],
                                     prep_bank[0:R, :].rearrange("p (b d) -> p b d", d=D),
                                     ACT.Copy).then_inc(prep_taken, 1)

            def take_xt(bt, c):
                i = bt * CPT + c
                act.wait_ge(prep_filled, xt_job(bt, c) + 1)
                if i >= 2:
                    act.wait_ge(diag_in[i % 2], 16 * SB * (i // 2))
                nc.scalar.activation(xt[:, i % 2, 0, :, 0:F],
                                     prep_bank[:, 0:SUBS * GW].rearrange("p (s m) -> p s m", m=GW)[:, :, 0:F],
                                     ACT.Copy).then_inc(xt_hi_done, 1)

            for k in range(len(GROUPS)):
                cast_hi(0, k)
                cast_mid(0, k)
            for k in range(XJ):
                take_x(0, k)
            take_a(0, 0)
            for s in range(UNITS + GOFF):
                bt, v = divmod(s, UPT)
                if s < UNITS:
                    n = len(unit_tiles(s % UPC))
                    rows = ROWS[unit_tiles(s % UPC)[0]]
                    act.wait_ge(product, q_of(s, n))
                    if s >= 3:
                        act.wait_ge(l1_used, s - 2)
                    nc.scalar.activation(z_hi[0:rows, s % 3, 0:n, :], z[0:rows, s % 2, 0:n, :],
                                         ACT.Copy).then_inc(rounded, 1)
                j = s - GOFF
                if j >= 0:
                    gt = j // (CPT * SUBS)
                    act.wait_ge(g_summed, j + 1)
                    if gt >= 2 and j % (CPT * SUBS) == 0:
                        act.wait_ge(s2_done, gt - 1)
                        act.wait_ge(z_copied, 2 * (gt - 1))
                    b0 = j % (CPT * SUBS) * SB
                    nc.scalar.activation(g[:, gt % 2, :, b0:b0 + SB],
                                         g_bank[:, 0:SB * GW].rearrange("p (b m) -> p m b", m=GW),
                                         ACT.Copy).then_inc(g_copied, 1)
                if s >= UPC + LAG - 1 and (s - UPC - LAG + 1) % UPC == 0 and (s - UPC - LAG + 1) // UPC < CHUNKS:
                    i = (s - UPC - LAG + 1) // UPC
                    act.wait_ge(l1_used, UPC * (i + 1))
                    if i:
                        act.wait_ge(xi_turned, i)
                    nc.scalar.activation(xi[:], l1_bank[:], ACT.Copy).then_inc(xi_copied, 1)
                if s >= UPC + LAG and (s - UPC - LAG) % UPC == 0 and (s - UPC - LAG) // UPC < CHUNKS:
                    i = (s - UPC - LAG) // UPC
                    act.wait_ge(xi_turned, i + 1)
                    if i >= 2:
                        act.wait_ge(g_summed, SUBS * (i - 1))
                    nc.scalar.activation(xit_hi[:, i % 2, :], xit_bank[:], ACT.Copy).then_inc(xit_hi_done, 1)
                if bt < TILES:
                    if v % UPC == 1:
                        take_xt(bt, v // UPC)
                    if v % UPC == 2 and v // UPC < CPT - 1:
                        take_a(bt, v // UPC + 1)
                if bt + 1 < TILES:
                    for k, at in enumerate(SPLIT_AT):
                        if v == at:
                            cast_hi(bt + 1, k)
                        if v == at + 1:
                            cast_mid(bt + 1, k)
                    if v in (X_AT, X_AT + 1):
                        take_x(bt + 1, v - X_AT)
                    if v == X_AT + 1:
                        take_a(bt + 1, 0)
                if s == UNITS + GOFF - 1:
                    act.wait_ge(mlp_in, 16 * 7)

            def relus(m, w, first, n, bias):
                lo, hi = GATE[m:m + 2]
                for k in range(n):
                    act.wait_ge(mlp_mm, MLP_MM * m + first + k + 1)
                    nc.scalar.activation(w[:, k, lo:hi], b_bank[(first + k) % 3][:, 0:hi - lo], ACT.Relu,
                                         bias=bias[:, k:k + 1]).then_inc(mlp_act, 1)

            for m in range(2):
                relus(m, h1, 0, H1T, bt1_sb)
                relus(m, h2, H1T, H2T, bt2_sb)

        @block.vector
        def _(dve):
            def rest_hi(bt, k):
                lo, hi = (x * D for x in GROUPS[k])
                dve.wait_ge(hi_cast, len(GROUPS) * bt + k + 1)
                nc.vector.tensor_sub(emb[:, bt, lo:hi], emb[:, bt, lo:hi], parts[:, 0, lo:hi]).then_inc(rest1, 1)

            def rest_mid(bt, k):
                lo, hi = (x * D for x in GROUPS[k])
                dve.wait_ge(mid_cast, len(GROUPS) * bt + k + 1)
                if bt:
                    dve.wait_ge(prep_filled, x_job(bt - 1, XJ - 1) + 1)
                nc.vector.tensor_sub(parts[:, 2, lo:hi], emb[:, bt, lo:hi], parts[:, 1, lo:hi]).then_inc(lo_cast, 1)

            nc.vector.memset(diag[:].bitcast(f32), 0.0).then_inc(zeroed, 1)
            nc.vector.memset(xt[:, :, 0, :, F:GW].bitcast(f32), 1.0).then_inc(zeroed, 1)
            nc.vector.memset(xt[:, :, 1, :, F:GW].bitcast(f32), 0.0).then_inc(zeroed, 1)
            dve.wait_ge(w0_in, 32)
            nc.vector.tensor_add(w0p[:], w0p[:], w0m[:]).then_inc(w0_summed, 1)
            dve.wait_ge(w0_summed, 1)
            nc.vector.tensor_copy(w0_hi[:], w0p[:]).then_inc(w0_summed, 1)
            dve.wait_ge(w0_summed, 2)
            nc.vector.tensor_sub(w0_lo[:], w0p[:], w0_hi[:].bitcast(f32)).then_inc(w0_split, 1)

            for k in range(len(GROUPS)):
                rest_hi(0, k)
                rest_mid(0, k)

            def low(u):
                n = len(unit_tiles(u % UPC))
                rows = ROWS[unit_tiles(u % UPC)[0]]
                dve.wait_ge(rounded, u + 1)
                if u >= 3:
                    dve.wait_ge(l1_used, u - 2)
                nc.vector.tensor_sub(z_lo[0:rows, u % 3, 0:n, :], z[0:rows, u % 2, 0:n, :],
                                     z_hi[0:rows, u % 3, 0:n, :].bitcast(f32)).then_inc(remainder, 1)

            for s in range(UNITS + GOFF):
                bt, v = divmod(s, UPT)
                if s < UNITS:
                    c = v // UPC
                    if s >= 2:
                        dve.wait_ge(remainder, s - 1)
                        dve.wait_ge(rounded, s - 1)
                    if s % UPC == 0:
                        dve.wait_ge(prep_taken, a_job(bt, c) + 1)
                    for j, t in enumerate(unit_tiles(s % UPC)):
                        q = q_of(s, j)
                        dve.wait_ge(selected, q + 1)
                        nc.vector.tensor_tensor(
                            z[0:ROWS[t], s % 2, j, :],
                            xa[0:ROWS[t], bt % 2, c * CB:(c + 1) * CB, :].rearrange("p b d -> p (b d)"),
                            b_bank[q % 3][0:ROWS[t], :], ALU.mult).then_inc(product, 1)
                if 1 <= s <= UNITS:
                    low(s - 1)
                if s >= UPC + LAG and (s - UPC - LAG) % UPC == 0 and (s - UPC - LAG) // UPC < CHUNKS:
                    i = (s - UPC - LAG) // UPC
                    dve.wait_ge(xit_hi_done, i + 1)
                    if i >= 2:
                        dve.wait_ge(g_summed, SUBS * (i - 1))
                    nc.vector.tensor_sub(xit_lo[:, i % 2, :], xit_bank[:],
                                         xit_hi[:, i % 2, :].bitcast(f32)).then_inc(xit_lo_done, 1)
                if bt < TILES and v % UPC == 1:
                    i = bt * CPT + v // UPC
                    dve.wait_ge(xt_hi_done, i + 1)
                    if i >= 2:
                        dve.wait_ge(diag_in[i % 2], 16 * SB * (i // 2))
                    nc.vector.tensor_sub(xt[:, i % 2, 1, :, 0:F],
                                         prep_bank[:, 0:SUBS * GW].rearrange("p (s m) -> p s m", m=GW)[:, :, 0:F],
                                         xt[:, i % 2, 0, :, 0:F].bitcast(f32)).then_inc(prep_taken, 1)
                if bt + 1 < TILES:
                    for k, at in enumerate(SPLIT_AT):
                        if v == at:
                            rest_hi(bt + 1, k)
                        if v == at + 1:
                            rest_mid(bt + 1, k)
                done = (s - GOFF - UPT - S2_STEPS + 1)
                if done >= 0 and done % UPT == 0 and done // UPT < TILES - 1:
                    copy_z(nc, dve, done // UPT, g, z1, z2, s2_bank, g_copied, s2_done, z_copied)
            copy_z(nc, dve, TILES - 1, g, z1, z2, s2_bank, g_copied, s2_done, z_copied)
            for m in range(2):
                lo, hi = GATE[m:m + 2]
                dve.wait_ge(mlp_mm, MLP_MM * (m + 1))
                nc.vector.tensor_copy(y_sb[:, lo:hi], l1_bank[0:1, lo:hi]).then_inc(y_copied, 1)

        @block.tensor
        def _(pe):
            def turn_x(bt, k):
                if bt or k:
                    pe.wait_ge(prep_taken, x_job(bt, k))
                if k == 0:
                    pe.wait_ge(lo_cast, len(GROUPS) * (bt + 1))
                for j in range(D // XJ):
                    last = nc.tensor.transpose(prep16[0:R, j * P:(j + 1) * P],
                                               parts[:, :, :].rearrange("p k (m d) -> p (k m) d", d=D)[:, :, k * D // XJ + j],
                                               id16[:])
                last.then_inc(prep_filled, 1)

            def columns(bt, c):
                return xs[:, bt % 2, c * CB:(c + 1) * CB, :].rearrange("p b d -> p (b d)")

            def fill_a(bt, c):
                pe.wait_ge(prep_taken, a_job(bt, c))
                nc.tensor.matmul(prep_bank[0:R, :], sel[:, PT, :], columns(bt, c),
                                 start=True, stop=True).then_inc(prep_filled, 1)

            def turn_a(bt, c):
                pe.wait_ge(prep_taken, xt_job(bt, c))
                for r in range(SUBS):
                    b0 = c * CB + r * SB
                    last = nc.tensor.transpose(prep_bank[:, r * GW:(r + 1) * GW],
                                               xa[0:GW, bt % 2, b0:b0 + SB, :].rearrange("p b d -> p (b d)"),
                                               id32[0:GW, 0:GW])
                last.then_inc(prep_filled, 1)

            def layer1(u):
                i, p = divmod(u, UPC)
                pe.wait_ge(remainder, u + 1)
                if p == 0 and i:
                    pe.wait_ge(xi_copied, i)
                for j, t in enumerate(unit_tiles(p)):
                    k = ROWS[t]
                    first, final = t == 0, t == PT - 1
                    nc.tensor.matmul(l1_bank[:], w0_hi[0:k, t, :], z_hi[0:k, u % 3, j, :], start=first, stop=False)
                    nc.tensor.matmul(l1_bank[:], w0_hi[0:k, t, :], z_lo[0:k, u % 3, j, :], start=False, stop=False)
                    last = nc.tensor.matmul(l1_bank[:], w0_lo[0:k, t, :], z_hi[0:k, u % 3, j, :],
                                            start=False, stop=final)
                last.then_inc(l1_used, 1)

            def turn_xi(i):
                pe.wait_ge(xi_copied, i + 1)
                if i:
                    pe.wait_ge(xit_lo_done, i)
                for r in range(SUBS):
                    last = nc.tensor.transpose(xit_bank[:, r * P:(r + 1) * P], xi[:, r * P:(r + 1) * P], id32[:])
                last.then_inc(xi_turned, 1)

            def g_block(j):
                i, r = divmod(j, SUBS)
                if r == 0:
                    pe.wait_ge(xit_lo_done, i + 1)
                    pe.wait_ge(diag_in[i % 2], 16 * SB * (i // 2 + 1))
                if j:
                    pe.wait_ge(g_copied, j)
                x_hi, x_lo = (diag[:, i % 2, h, r, :, :].rearrange("p b m -> p (b m)") for h in range(2))
                y_hi, y_lo = (w[:, i % 2, r * P:(r + 1) * P] for w in (xit_hi, xit_lo))
                o = g_bank[:, 0:SB * GW]
                nc.tensor.matmul(o, y_hi, x_hi, start=True, stop=False)
                nc.tensor.matmul(o, y_hi, x_lo, start=False, stop=False)
                nc.tensor.matmul(o, y_lo, x_hi, start=False, stop=True).then_inc(g_summed, 1)

            def layer2(bt, first, end):
                if first == 0:
                    pe.wait_ge(g_copied, CPT * SUBS * (bt + 1))
                    if bt:
                        pe.wait_ge(z_copied, 2 * bt)
                for m in range(first, end):
                    last = nc.tensor.matmul(s2_bank[:, 0:P], w1_sb[:, m, :], g[:, bt % 2, m, :],
                                            start=m == 0, stop=m == F - 1)
                if end == F:
                    last.then_inc(s2_done, 1)

            def mlp1(m, k):
                lo, hi = GATE[m:m + 2]
                used = (H1T + H2T) * m + k
                if used >= 3:
                    pe.wait_ge(mlp_act, used - 2)
                o = b_bank[k % 3][:, 0:hi - lo]
                h = slice(k * P, (k + 1) * P)
                nc.tensor.matmul(o, wt1c_sb[:, h], dt_sb[:, lo:hi], start=True, stop=False)
                nc.tensor.matmul(o, wt1_sb[:, 0, h], z1[:, lo:hi], start=False, stop=False)
                nc.tensor.matmul(o, wt1_sb[:, 1, h], z2[:, lo:hi], start=False, stop=True).then_inc(mlp_mm, 1)

            def mlp2(m):
                lo, hi = GATE[m:m + 2]
                pe.wait_ge(mlp_act, (H1T + H2T) * m + H1T)
                for k in range(H2T):
                    for kk in range(H1T):
                        last = nc.tensor.matmul(b_bank[(H1T + k) % 3][:, 0:hi - lo], wt2_sb[:, kk, k * P:(k + 1) * P],
                                                h1[:, kk, lo:hi], start=kk == 0, stop=kk == H1T - 1)
                    last.then_inc(mlp_mm, 1)

            def mlp3(m):
                lo, hi = GATE[m:m + 2]
                pe.wait_ge(mlp_act, (H1T + H2T) * (m + 1))
                if m:
                    pe.wait_ge(y_copied, 1)
                for k in range(H2T):
                    last = nc.tensor.matmul(l1_bank[0:1, lo:hi], wt3_sb[:, k:k + 1], h2[:, k, lo:hi],
                                            start=k == 0, stop=k == H2T - 1)
                last.then_inc(mlp_mm, 1)

            pe.wait_ge(consts_in, 48)
            for k in range(XJ):
                turn_x(0, k)
            fill_a(0, 0)
            pe.wait_ge(w0_split, 1)
            pe.wait_ge(w1_in, 16)
            share = [F * k // S2_STEPS for k in range(S2_STEPS + 1)]
            for s in range(UNITS + GOFF):
                bt, v = divmod(s, UPT)
                if s < UNITS:
                    for j, t in enumerate(unit_tiles(s % UPC)):
                        q = q_of(s, j)
                        if q >= 3:
                            pe.wait_ge(product, q - 2)
                        nc.tensor.matmul(b_bank[q % 3][0:ROWS[t], :], sel[:, t, 0:ROWS[t]], columns(bt, v // UPC),
                                         start=True, stop=True).then_inc(selected, 1)
                if s == UNITS:
                    pe.wait_ge(mlp_in, 16 * 7)
                if LAG <= s < UNITS + LAG:
                    layer1(s - LAG)
                if s >= UPC + LAG and (s - UPC - LAG) % UPC == 0 and (s - UPC - LAG) // UPC < CHUNKS:
                    turn_xi((s - UPC - LAG) // UPC)
                if s >= GOFF:
                    g_block(s - GOFF)
                tile, k = divmod(s - GOFF - UPT, UPT)
                if tile >= 0 and k < S2_STEPS:
                    layer2(tile, share[k], share[k + 1])
                if bt < TILES:
                    if v % UPC == 1:
                        turn_a(bt, v // UPC)
                    if v % UPC == 2 and v // UPC < CPT - 1:
                        fill_a(bt, v // UPC + 1)
                if bt + 1 < TILES:
                    if v in (X_AT, X_AT + 1):
                        turn_x(bt + 1, v - X_AT)
                    if v == X_AT + 1:
                        fill_a(bt + 1, 0)
            pe.wait_ge(z_copied, 2 * (TILES - 1))
            for k in range(H1T):
                mlp1(0, k)
            layer2(TILES - 1, 0, F)
            mlp2(0)
            mlp3(0)
            pe.wait_ge(z_copied, 2 * TILES)
            for k in range(H1T):
                mlp1(1, k)
            mlp2(1)
            mlp3(1)


def copy_z(nc, dve, bt, g, z1, z2, s2_bank, g_copied, s2_done, z_copied):
    cols = slice(bt * P, (bt + 1) * P)
    dve.wait_ge(g_copied, CPT * SUBS * (bt + 1))
    nc.vector.tensor_copy(z1[:, cols], g[:, bt % 2, F, :]).then_inc(z_copied, 1)
    dve.wait_ge(s2_done, bt + 1)
    nc.vector.tensor_copy(z2[:, cols], s2_bank[:, 0:P]).then_inc(z_copied, 1)


def _pair_rows():
    n = np.arange(F)
    pair = np.zeros((PT, R), np.int64)
    mirror = np.full((PT, R), -1, np.int64)
    for k in range(SHIFTS):
        t, j = divmod(k, PER)
        m = (n + k) % F
        pair[t, j * F:(j + 1) * F] = n * F + m
        if k:
            mirror[t, j * F:(j + 1) * F] = m * F + n
    return pair, mirror


def _selections():
    s = np.zeros((R, PT + 1, R), np.float32)
    for t in range(PT + 1):
        for j in range(PER):
            for n in range(F):
                m = n if t == PT else (n + PER * t + j) % F
                s[m::F, t, j * F + n] = 1.0
    return s


def kernel(**inputs):
    import concourse.bacc as bacc
    import ml_dtypes
    from concourse.bass_utils import run_bass_kernel_spmd

    a = {k: np.asarray(v) for k, v in inputs.items()}
    pair, mirror = _pair_rows()
    w0 = a["L0_rec_W0"]
    w0_pair = np.zeros((PT, R, O), w0.dtype)
    w0_mirror = np.zeros((PT, R, O), w0.dtype)
    for t in range(PT):
        w0_pair[t, :ROWS[t]] = w0[pair[t, :ROWS[t]]]
        has = mirror[t] >= 0
        w0_mirror[t, has] = w0[mirror[t][has]]
    arrays = {
        "ids": np.ascontiguousarray(a["ids"].reshape(TILES, P, F).transpose(1, 0, 2)),
        "dense_t": np.ascontiguousarray(a["dense_ctx"].T),
        "w0_pair": w0_pair,
        "w0_mirror": w0_mirror,
        "w1": a["L0_rec_W1"],
        "wt1": a["W_top1"],
        "bt1": np.ascontiguousarray(a["b_top1"].reshape(H1T, P).T),
        "wt2": a["W_top2"],
        "bt2": np.ascontiguousarray(a["b_top2"].reshape(H2T, P).T),
        "wt3": np.ascontiguousarray(a["W_top3"].reshape(H2T, P).T),
        "select": _selections().astype(ml_dtypes.bfloat16),
        "ident16": np.eye(P, dtype=ml_dtypes.bfloat16),
        "ident32": np.eye(P, dtype=np.float32),
    }
    arrays.update({f"tbl_{f}": a[f"tbl_{f}"] for f in range(F)})
    nc = bacc.Bacc("TRN2", target_bir_lowering=False, num_devices=1)
    aps = {k: nc.dram_tensor(k, v.shape, mybir.dt.from_np(v.dtype), kind="ExternalInput").ap()
           for k, v in arrays.items()}
    tables = [aps.pop(f"tbl_{f}") for f in range(F)]
    out = nc.dram_tensor("y", (B, 1), mybir.dt.float32, kind="ExternalOutput").ap()
    build(nc, tables=tables, out=out, **aps)
    return run_bass_kernel_spmd(nc, [arrays], core_ids=[0]).results[0]["y"]
```

```python
from contextlib import ExitStack

import concourse.bass as bass
import concourse.mybir as mybir
import numpy as np

F = 39
D = 16
B = 512
O = 128
P = 128
TILES = B // P
PARTS = 3
R = PARTS * F
PAIRS = F * (F + 1) // 2
PT = -(-PAIRS // P)
REST = PAIRS - (PT - 1) * P
REST_AT = (0, F, 2 * F)
REST_LO = 64
REST_ROWS = 96
ROWS = [P] * (PT - 1) + [REST_ROWS]
assert REST <= F and REST_AT[1] >= 32 and REST_AT[1] + REST <= REST_LO <= REST_AT[2] and REST_AT[2] + REST <= REST_ROWS
CH = 512
CB = CH // D
CPT = P // CB
CHUNKS = TILES * CPT
SUBS = CH // P
SB = P // D
GW = F + 1
STEPS = CHUNKS * PT
SPT = CPT * PT
LAG = 5
LEAD = 1
RING = LAG + 2
GROUPS = [(0, 13), (13, 26), (26, F)]
COPY_XI = PT - 1 + LAG
TURN_XI = COPY_XI + 2
G_AT = [TURN_XI + 4 + 2 * r for r in range(CH // P)]
TURN_A = 1
FILL_A = 3
LAST = STEPS - PT + G_AT[-1] + 1
SPLIT_AT = [8, 14, 20]
X_AT = 24
A_AT = X_AT + 2
S2_AT = SPT - PT + G_AT[-1] + 1
S2_STEPS = [SPT - 2] * (TILES - 2) + [12]
MLP_AT = S2_AT + SPT * (TILES - 2) + 15
HID1, HID2, DC = 512, 256, 16
H1T, H2T = HID1 // P, HID2 // P
XJ = 2
PREP = XJ + 2 * CPT


def chunk_at(s, offset):
    i, rest = divmod(s - offset, PT)
    return i if rest == 0 and 0 <= i < CHUNKS else None


def build(nc, ids, tables, dense_t, w0_pair, w0_mirror, w1, wt1, bt1, wt2, bt2, wt3, select, ident16, ident32, out):
    f32, bf16, f32r, i32 = mybir.dt.float32, mybir.dt.bfloat16, mybir.dt.float32r, mybir.dt.int32
    ACT, ALU = mybir.ActivationFunctionType, mybir.AluOpType
    ctx = ExitStack()
    with ctx:
        def sb(name, shape, dt=f32):
            return ctx.enter_context(nc.sbuf_tensor(name, shape, dt))

        def bank(name):
            return ctx.enter_context(nc.psum_tensor(name, [P, 512], f32))

        def sem(name):
            return ctx.enter_context(nc.semaphore(name))

        ids_sb = sb("ids_sb", [P, TILES, F], i32)
        emb = sb("emb", [P, TILES, F * D])
        parts = sb("parts", [P, PARTS, F * D], bf16)
        xs = sb("xs", [R, 2, P, D], bf16)
        xa = sb("xa", [P, 2, P, D])
        sel = sb("sel", [R, PT + 1, P], bf16)
        id16 = sb("id16", [P, P], bf16)
        id32 = sb("id32", [P, P])
        z = sb("z", [P, 3, CH])
        z_hi = sb("z_hi", [P, RING, CH], f32r)
        z_lo = sb("z_lo", [P, RING, CH], f32r)
        w0p = sb("w0p", [P, PT, O])
        w0m = sb("w0m", [P, PT, O])
        w0_hi = sb("w0_hi", [P, PT, O], f32r)
        w0_lo = sb("w0_lo", [P, PT, O], f32r)
        w0_rest = sb("w0_rest", [REST_ROWS, O], f32r)
        xi = sb("xi", [O, CH])
        xit_hi = sb("xit_hi", [P, 2, CH], f32r)
        xit_lo = sb("xit_lo", [P, 2, CH], f32r)
        xt = sb("xt", [P, 2, 2, SUBS, GW], f32r)
        diag = sb("diag", [P, 2, 2, SUBS, SB, GW], f32r)
        g = sb("g", [O, 2, GW, P])
        w1_sb = sb("w1_sb", [O, F, O])
        z1 = sb("z1", [O, B])
        z2 = sb("z2", [O, B])
        dt_sb = sb("dt_sb", [DC, B])
        wt1_sb = sb("wt1_sb", [P, 2, HID1])
        wt1c_sb = sb("wt1c_sb", [DC, HID1])
        wt2_sb = sb("wt2_sb", [P, H1T, HID2])
        wt3_sb = sb("wt3_sb", [P, H2T])
        bt1_sb = sb("bt1_sb", [P, H1T])
        bt2_sb = sb("bt2_sb", [P, H2T])
        hidden = g[:, 0, :, :].rearrange("p m b -> p (m b)")
        h1 = hidden[:, 0:H1T * B].rearrange("p (k b) -> p k b", b=B)
        h2 = hidden[:, H1T * B:(H1T + H2T) * B].rearrange("p (k b) -> p k b", b=B)
        y_sb = sb("y_sb", [1, B])

        b_bank = [bank(f"b_bank{j}") for j in range(3)]
        l1_bank = [bank(f"l1_bank{j}") for j in range(2)]
        turn_bank = bank("turn_bank")
        g_bank = bank("g_bank")
        s2_bank = bank("s2_bank")
        turn16 = turn_bank[:, :].bitcast(bf16)

        ids_in = sem("ids_in")
        consts_in = sem("consts_in")
        w0_in = sem("w0_in")
        w1_in = sem("w1_in")
        mlp_in = sem("mlp_in")
        gathered = [[sem(f"gathered{bt}_{k}") for k in range(len(GROUPS))] for bt in range(TILES)]
        hi_cast = sem("hi_cast")
        rest1 = sem("rest1")
        mid_cast = sem("mid_cast")
        lo_cast = sem("lo_cast")
        turn_filled = sem("turn_filled")
        turn_taken = sem("turn_taken")
        xt_hi_done = sem("xt_hi_done")
        w0_summed = sem("w0_summed")
        w0_split = sem("w0_split")
        zeroed = sem("zeroed")
        selected = sem("selected")
        product = sem("product")
        rounded = sem("rounded")
        remainder = sem("remainder")
        l1_used = sem("l1_used")
        xi_copied = sem("xi_copied")
        xit_hi_done = sem("xit_hi_done")
        diag_in = [sem(f"diag_in{j}") for j in range(2)]
        g_summed = sem("g_summed")
        g_copied = sem("g_copied")
        s2_done = sem("s2_done")
        z_copied = sem("z_copied")
        mlp_mm = sem("mlp_mm")
        mlp_act = sem("mlp_act")
        y_copied = sem("y_copied")
        y_out = sem("y_out")

        block = ctx.enter_context(nc.Block())

        order = [("x", 0, 0), ("x", 0, 1), ("a", 0, 0)]
        for s in range(LAST):
            bt, v = divmod(s, SPT)
            if chunk_at(s, TURN_A) is not None:
                order.append(("xt", s // PT, 0))
            if chunk_at(s, FILL_A) is not None and (s // PT + 1) % CPT:
                order.append(("a", s // PT + 1, 0))
            if bt + 1 < TILES and v in (X_AT, X_AT + 1):
                order.append(("x", bt + 1, v - X_AT))
            if bt + 1 < TILES and v == A_AT:
                order.append(("a", CPT * (bt + 1), 0))
            if chunk_at(s, TURN_XI) is not None:
                order.append(("xi", chunk_at(s, TURN_XI), 0))
        fill = {job: n for n, job in enumerate(order)}

        def g_place(j):
            return l1_bank[0] if j >= SUBS * (CHUNKS - 1) and j % 2 else g_bank

        GATE = [0, 3 * P, B]
        MLP_MM = H1T + H2T + 1
        mlp_bank = [*b_bank, s2_bank, *b_bank[:H2T]]

        @block.gpsimd
        def _(pool):
            pool.wait_ge(ids_in, 16)
            for bt in range(TILES):
                for k, (lo, hi) in enumerate(GROUPS):
                    for f in range(lo, hi):
                        nc.gpsimd.indirect_dma_start(
                            emb[:, bt, f * D:(f + 1) * D], None, tables[f],
                            bass.IndirectOffsetOnAxis(ids_sb[:, bt, f:f + 1], 0)).then_inc(gathered[bt][k], 16)

        @block.sync
        def _(sp):
            sp.dma_start(ids_sb[:], ids).then_inc(ids_in, 16)
            sp.dma_start(w0p[:], w0_pair.rearrange("t p o -> p t o")).then_inc(w0_in, 16)
            sp.dma_start(w0m[:], w0_mirror.rearrange("t p o -> p t o")).then_inc(w0_in, 16)
            sp.dma_start(sel[:], select).then_inc(consts_in, 16)
            sp.dma_start(id16[:], ident16).then_inc(consts_in, 16)
            sp.dma_start(id32[:], ident32).then_inc(consts_in, 16)
            sp.dma_start(w1_sb[:], w1.rearrange("(m n) o -> n m o", n=O)).then_inc(w1_in, 16)
            sp.dma_start(wt1_sb[:], wt1[0:2 * P, :].rearrange("(k p) h -> p k h", p=P)).then_inc(mlp_in, 16)
            sp.dma_start(wt1c_sb[:], wt1[2 * P:2 * P + DC, :]).then_inc(mlp_in, 16)
            sp.dma_start(wt2_sb[:], wt2.rearrange("(k p) h -> p k h", p=P)).then_inc(mlp_in, 16)
            sp.dma_start(wt3_sb[:], wt3).then_inc(mlp_in, 16)
            sp.dma_start(bt1_sb[:], bt1).then_inc(mlp_in, 16)
            sp.dma_start(bt2_sb[:], bt2).then_inc(mlp_in, 16)
            sp.dma_start(dt_sb[:], dense_t).then_inc(mlp_in, 16)
            sp.wait_ge(zeroed, 3)
            for i in range(CHUNKS):
                sp.wait_ge(turn_taken, fill["xt", i, 0] + 1)
                if i >= 2:
                    sp.wait_ge(g_summed, SUBS * (i - 1))
                for b in range(SB):
                    sp.dma_start(diag[b * D:(b + 1) * D, i % 2, :, :, b, :].bitcast(f32),
                                 xt[b * D:(b + 1) * D, i % 2, :, :, :].bitcast(f32)).then_inc(diag_in[i % 2], 16)
            sp.wait_ge(y_copied, 2)
            sp.dma_start(out.rearrange("b o -> o b"), y_sb[:]).then_inc(y_out, 16)
            sp.wait_ge(y_out, 16)

        @block.scalar
        def _(act):
            def cast_hi(bt, k):
                lo, hi = (x * D for x in GROUPS[k])
                act.wait_ge(gathered[bt][k], 16 * (GROUPS[k][1] - GROUPS[k][0]))
                if bt:
                    act.wait_ge(turn_filled, fill["x", bt - 1, XJ - 1] + 1)
                nc.scalar.activation(parts[:, 0, lo:hi], emb[:, bt, lo:hi], ACT.Copy).then_inc(hi_cast, 1)

            def cast_mid(bt, k):
                lo, hi = (x * D for x in GROUPS[k])
                act.wait_ge(rest1, len(GROUPS) * bt + k + 1)
                nc.scalar.activation(parts[:, 1, lo:hi], emb[:, bt, lo:hi], ACT.Copy).then_inc(mid_cast, 1)

            def take_x(bt, k):
                act.wait_ge(turn_filled, fill["x", bt, k] + 1)
                nc.scalar.activation(
                    xs[:, bt % 2, :, k * D // XJ:(k + 1) * D // XJ],
                    turn16[0:R, :].rearrange("p (d b) -> p b d", b=P),
                    ACT.Copy).then_inc(turn_taken, 1)

            def take_a(i):
                bt, c = divmod(i, CPT)
                act.wait_ge(turn_filled, fill["a", i, 0] + 1)
                nc.scalar.activation(xa[:, bt % 2, c * CB:(c + 1) * CB, :],
                                     turn_bank[:].rearrange("p (b d) -> p b d", d=D),
                                     ACT.Copy).then_inc(turn_taken, 1)

            def take_xt(i):
                act.wait_ge(turn_filled, fill["xt", i, 0] + 1)
                if i >= 2:
                    act.wait_ge(diag_in[i % 2], 16 * SB * (i // 2))
                nc.scalar.activation(xt[:, i % 2, 0, :, 0:F],
                                     turn_bank[:, 0:SUBS * GW].rearrange("p (s m) -> p s m", m=GW)[:, :, 0:F],
                                     ACT.Copy).then_inc(xt_hi_done, 1)

            for k in range(len(GROUPS)):
                cast_hi(0, k)
                cast_mid(0, k)
            for k in range(XJ):
                take_x(0, k)
            take_a(0)

            def round_z(s):
                rows = ROWS[s % PT]
                act.wait_ge(product, s + 1)
                if s >= RING:
                    act.wait_ge(l1_used, s - RING + 1)
                nc.scalar.activation(z_hi[0:rows, s % RING, :], z[0:rows, s % 3, :], ACT.Copy).then_inc(rounded, 1)

            def take_g(j):
                bt, block = divmod(j, CPT * SUBS)
                act.wait_ge(g_summed, j + 1)
                if bt >= 2 and block == 0:
                    act.wait_ge(s2_done, bt - 1)
                    act.wait_ge(z_copied, 2 * (bt - 1))
                nc.scalar.activation(g[:, bt % 2, :, block * SB:(block + 1) * SB],
                                     g_place(j)[:, 0:SB * GW].rearrange("p (b m) -> p m b", m=GW),
                                     ACT.Copy).then_inc(g_copied, 1)

            def take_xi(i):
                act.wait_ge(l1_used, PT * (i + 1))
                if i:
                    act.wait_ge(turn_filled, fill["xi", i - 1, 0] + 1)
                nc.scalar.activation(xi[:], l1_bank[i % 2][:], ACT.Copy).then_inc(xi_copied, 1)

            def round_xit(i):
                act.wait_ge(turn_filled, fill["xi", i, 0] + 1)
                if i >= 2:
                    act.wait_ge(g_summed, SUBS * (i - 1))
                nc.scalar.activation(xit_hi[:, i % 2, :], turn_bank[:], ACT.Copy).then_inc(xit_hi_done, 1)

            def relu(m, k):
                lo, hi = GATE[m:m + 2]
                if m == 0 and k == 0:
                    act.wait_ge(mlp_in, 16 * 7)
                    act.wait_ge(s2_done, TILES - 1)
                act.wait_ge(mlp_mm, MLP_MM * m + k + 1)
                h, bias, j = (h1, bt1_sb, k) if k < H1T else (h2, bt2_sb, k - H1T)
                nc.scalar.activation(h[:, j, lo:hi], mlp_bank[k][:, 0:hi - lo], ACT.Relu,
                                     bias=bias[:, j:j + 1]).then_inc(mlp_act, 1)

            for s in range(LAST):
                bt, v = divmod(s, SPT)
                if s < STEPS:
                    round_z(s)
                for r, at in enumerate(G_AT):
                    if (i := chunk_at(s, at)) is not None:
                        take_g(SUBS * i + r)
                if (i := chunk_at(s, COPY_XI)) is not None:
                    take_xi(i)
                if (i := chunk_at(s, TURN_XI)) is not None:
                    round_xit(i)
                if (i := chunk_at(s, TURN_A)) is not None:
                    take_xt(i)
                if (i := chunk_at(s, FILL_A)) is not None and (i + 1) % CPT:
                    take_a(i + 1)
                if bt + 1 < TILES:
                    for k, at in enumerate(SPLIT_AT):
                        if v == at:
                            cast_hi(bt + 1, k)
                        if v == at + 1:
                            cast_mid(bt + 1, k)
                    if v in (X_AT, X_AT + 1):
                        take_x(bt + 1, v - X_AT)
                    if v == A_AT:
                        take_a(CPT * (bt + 1))
                if s >= MLP_AT and (s - MLP_AT) % 2 == 0 and (s - MLP_AT) // 2 < H1T + H2T:
                    relu(0, (s - MLP_AT) // 2)

            for k in range(H1T + H2T):
                relu(1, k)

        @block.vector
        def _(dve):
            def rest_hi(bt, k):
                lo, hi = (x * D for x in GROUPS[k])
                dve.wait_ge(hi_cast, len(GROUPS) * bt + k + 1)
                nc.vector.tensor_sub(emb[:, bt, lo:hi], emb[:, bt, lo:hi], parts[:, 0, lo:hi]).then_inc(rest1, 1)

            def rest_mid(bt, k):
                lo, hi = (x * D for x in GROUPS[k])
                dve.wait_ge(mid_cast, len(GROUPS) * bt + k + 1)
                if bt:
                    dve.wait_ge(turn_filled, fill["x", bt - 1, XJ - 1] + 1)
                nc.vector.tensor_sub(parts[:, 2, lo:hi], emb[:, bt, lo:hi], parts[:, 1, lo:hi]).then_inc(lo_cast, 1)

            nc.vector.memset(diag[:].bitcast(f32), 0.0).then_inc(zeroed, 1)
            nc.vector.memset(xt[:, :, 0, :, F:GW].bitcast(f32), 1.0).then_inc(zeroed, 1)
            nc.vector.memset(xt[:, :, 1, :, F:GW].bitcast(f32), 0.0).then_inc(zeroed, 1)
            dve.wait_ge(w0_in, 32)
            nc.vector.tensor_add(w0p[:], w0p[:], w0m[:]).then_inc(w0_summed, 1)
            dve.wait_ge(w0_summed, 1)
            nc.vector.tensor_copy(w0_hi[:], w0p[:]).then_inc(w0_summed, 1)
            dve.wait_ge(w0_summed, 2)
            nc.vector.tensor_sub(w0_lo[:], w0p[:], w0_hi[:].bitcast(f32)).then_inc(w0_summed, 1)
            dve.wait_ge(w0_summed, 3)
            for lo in range(0, REST_ROWS, 32):
                w = w0_lo if lo == 32 else w0_hi
                nc.vector.tensor_copy(w0_rest[lo:lo + 32, :], w[lo:lo + 32, PT - 1, :]).then_inc(w0_split, 1)

            for k in range(len(GROUPS)):
                rest_hi(0, k)
                rest_mid(0, k)

            def multiply(s):
                i, t = divmod(s, PT)
                bt, c = divmod(i, CPT)
                rows = ROWS[t]
                if s >= 3:
                    dve.wait_ge(remainder, s - 2)
                    dve.wait_ge(rounded, s - 2)
                if t == 0:
                    dve.wait_ge(turn_taken, fill["a", i, 0] + 1)
                dve.wait_ge(selected, s + 1)
                nc.vector.tensor_tensor(z[0:rows, s % 3, :],
                                        xa[0:rows, bt % 2, c * CB:(c + 1) * CB, :].rearrange("p b d -> p (b d)"),
                                        b_bank[s % 3][0:rows, :], ALU.mult).then_inc(product, 1)

            def rest_z(s):
                rows = ROWS[s % PT]
                dve.wait_ge(rounded, s + 1)
                if s >= RING:
                    dve.wait_ge(l1_used, s - RING + 1)
                low = z_lo if s % PT < PT - 1 else z_hi
                first = 0 if s % PT < PT - 1 else REST_LO
                nc.vector.tensor_sub(low[first:rows, s % RING, :], z[first:rows, s % 3, :],
                                     z_hi[first:rows, s % RING, :].bitcast(f32)).then_inc(remainder, 1)

            def rest_xit(i):
                dve.wait_ge(xit_hi_done, i + 1)
                if i >= 2:
                    dve.wait_ge(g_summed, SUBS * (i - 1))
                nc.vector.tensor_sub(xit_lo[:, i % 2, :], turn_bank[:],
                                     xit_hi[:, i % 2, :].bitcast(f32)).then_inc(turn_taken, 1)

            def rest_xt(i):
                dve.wait_ge(xt_hi_done, i + 1)
                if i >= 2:
                    dve.wait_ge(diag_in[i % 2], 16 * SB * (i // 2))
                nc.vector.tensor_sub(xt[:, i % 2, 1, :, 0:F],
                                     turn_bank[:, 0:SUBS * GW].rearrange("p (s m) -> p s m", m=GW)[:, :, 0:F],
                                     xt[:, i % 2, 0, :, 0:F].bitcast(f32)).then_inc(turn_taken, 1)

            def copy_z(bt):
                cols = slice(bt * P, (bt + 1) * P)
                dve.wait_ge(g_copied, CPT * SUBS * (bt + 1))
                nc.vector.tensor_copy(z1[:, cols], g[:, bt % 2, F, :]).then_inc(z_copied, 1)
                dve.wait_ge(s2_done, bt + 1)
                nc.vector.tensor_copy(z2[:, cols], s2_bank[:, 0:P]).then_inc(z_copied, 1)

            for s in range(LAST):
                bt, v = divmod(s, SPT)
                if s < STEPS:
                    multiply(s)
                if 1 <= s <= STEPS:
                    rest_z(s - 1)
                if (i := chunk_at(s, TURN_XI + 1)) is not None:
                    rest_xit(i)
                if (i := chunk_at(s, TURN_A + 1)) is not None:
                    rest_xt(i)
                if bt + 1 < TILES:
                    for k, at in enumerate(SPLIT_AT):
                        if v == at:
                            rest_hi(bt + 1, k)
                        if v == at + 1:
                            rest_mid(bt + 1, k)
                tile, k = divmod(s - S2_AT, SPT)
                if 0 <= tile < TILES - 1 and k == S2_STEPS[tile]:
                    copy_z(tile)
            copy_z(TILES - 1)
            for m in range(2):
                lo, hi = GATE[m:m + 2]
                dve.wait_ge(mlp_mm, MLP_MM * (m + 1))
                nc.vector.tensor_copy(y_sb[:, lo:hi], l1_bank[1][0:1, lo:hi]).then_inc(y_copied, 1)

        @block.tensor
        def _(pe):
            def turn_free(*job):
                if fill[job]:
                    pe.wait_ge(turn_taken, fill[job])

            def turn_x(bt, k):
                turn_free("x", bt, k)
                if k == 0:
                    pe.wait_ge(lo_cast, len(GROUPS) * (bt + 1))
                for j in range(D // XJ):
                    last = nc.tensor.transpose(turn16[0:R, j * P:(j + 1) * P],
                                               parts[:, :, :].rearrange("p k (m d) -> p (k m) d", d=D)[:, :, k * D // XJ + j],
                                               id16[:])
                last.then_inc(turn_filled, 1)

            def columns(bt, c):
                return xs[:, bt % 2, c * CB:(c + 1) * CB, :].rearrange("p b d -> p (b d)")

            def fill_a(i):
                turn_free("a", i, 0)
                nc.tensor.matmul(turn_bank[:], sel[:, PT, :], columns(i // CPT, i % CPT),
                                 start=True, stop=True).then_inc(turn_filled, 1)

            def turn_a(i):
                bt, c = divmod(i, CPT)
                turn_free("xt", i, 0)
                for r in range(SUBS):
                    b0 = c * CB + r * SB
                    last = nc.tensor.transpose(turn_bank[:, r * GW:(r + 1) * GW],
                                               xa[0:GW, bt % 2, b0:b0 + SB, :].rearrange("p b d -> p (b d)"),
                                               id32[0:GW, 0:GW])
                last.then_inc(turn_filled, 1)

            def select(s):
                i, t = divmod(s, PT)
                bt, c = divmod(i, CPT)
                if s >= 3:
                    pe.wait_ge(product, s - 2)
                if t == 0:
                    pe.wait_ge(turn_taken, fill["x", bt, XJ - 1] + 1)
                nc.tensor.matmul(b_bank[s % 3][0:ROWS[t], :], sel[:, t, 0:ROWS[t]], columns(bt, c),
                                 start=True, stop=True).then_inc(selected, 1)

            def layer1(s):
                i, t = divmod(s, PT)
                bank, slot = l1_bank[i % 2], s % RING
                pe.wait_ge(remainder, s + 1)
                if t == 0 and i >= 2:
                    pe.wait_ge(xi_copied, i - 1)
                if t == PT - 1:
                    nc.tensor.matmul(bank[:], w0_rest[:], z_hi[0:REST_ROWS, slot, :],
                                     start=False, stop=True).then_inc(l1_used, 1)
                else:
                    nc.tensor.matmul(bank[:], w0_hi[:, t, :], z_hi[:, slot, :], start=t == 0, stop=False)
                    nc.tensor.matmul(bank[:], w0_hi[:, t, :], z_lo[:, slot, :], start=False, stop=False)
                    nc.tensor.matmul(bank[:], w0_lo[:, t, :], z_hi[:, slot, :],
                                     start=False, stop=False).then_inc(l1_used, 1)

            def turn_xi(i):
                pe.wait_ge(xi_copied, i + 1)
                turn_free("xi", i, 0)
                for r in range(SUBS):
                    last = nc.tensor.transpose(turn_bank[:, r * P:(r + 1) * P], xi[:, r * P:(r + 1) * P], id32[:])
                last.then_inc(turn_filled, 1)

            def g_block(j):
                i, r = divmod(j, SUBS)
                if r == 0:
                    pe.wait_ge(turn_taken, fill["xi", i, 0] + 1)
                    pe.wait_ge(diag_in[i % 2], 16 * SB * (i // 2 + 1))
                if j >= SUBS * (CHUNKS - 1) + 2:
                    pe.wait_ge(g_copied, j - 1)
                elif j and j != SUBS * (CHUNKS - 1) + 1:
                    pe.wait_ge(g_copied, j)
                x_hi, x_lo = (diag[:, i % 2, h, r, :, :].rearrange("p b m -> p (b m)") for h in range(2))
                y_hi, y_lo = (w[:, i % 2, r * P:(r + 1) * P] for w in (xit_hi, xit_lo))
                o = g_place(j)[:, 0:SB * GW]
                nc.tensor.matmul(o, y_hi, x_hi, start=True, stop=False)
                nc.tensor.matmul(o, y_hi, x_lo, start=False, stop=False)
                nc.tensor.matmul(o, y_lo, x_hi, start=False, stop=True).then_inc(g_summed, 1)

            def layer2(bt, first, end):
                if first == end:
                    return
                if first == 0:
                    pe.wait_ge(g_copied, CPT * SUBS * (bt + 1))
                    if bt:
                        pe.wait_ge(z_copied, 2 * bt)
                for m in range(first, end):
                    last = nc.tensor.matmul(s2_bank[:, 0:P], w1_sb[:, m, :], g[:, bt % 2, m, :],
                                            start=m == 0, stop=m == F - 1)
                if end == F:
                    last.then_inc(s2_done, 1)

            def mlp1(m, k, first=True, second=True):
                lo, hi = GATE[m:m + 2]
                o = mlp_bank[k][:, 0:hi - lo]
                h = slice(k * P, (k + 1) * P)
                if first:
                    if m:
                        pe.wait_ge(mlp_act, (H1T + H2T))
                    nc.tensor.matmul(o, wt1c_sb[:, h], dt_sb[:, lo:hi], start=True, stop=False)
                    nc.tensor.matmul(o, wt1_sb[:, 0, h], z1[:, lo:hi], start=False, stop=False)
                if second:
                    nc.tensor.matmul(o, wt1_sb[:, 1, h], z2[:, lo:hi], start=False, stop=True).then_inc(mlp_mm, 1)

            def mlp2(m, k):
                lo, hi = GATE[m:m + 2]
                pe.wait_ge(mlp_act, (H1T + H2T) * m + H1T)
                for kk in range(H1T):
                    last = nc.tensor.matmul(mlp_bank[H1T + k][:, 0:hi - lo], wt2_sb[:, kk, k * P:(k + 1) * P],
                                            h1[:, kk, lo:hi], start=kk == 0, stop=kk == H1T - 1)
                last.then_inc(mlp_mm, 1)

            def mlp3(m):
                lo, hi = GATE[m:m + 2]
                pe.wait_ge(mlp_act, (H1T + H2T) * (m + 1))
                if m:
                    pe.wait_ge(y_copied, 1)
                for k in range(H2T):
                    last = nc.tensor.matmul(l1_bank[1][0:1, lo:hi], wt3_sb[:, k:k + 1], h2[:, k, lo:hi],
                                            start=k == 0, stop=k == H2T - 1)
                last.then_inc(mlp_mm, 1)

            pe.wait_ge(consts_in, 48)
            for k in range(XJ):
                turn_x(0, k)
            fill_a(0)
            pe.wait_ge(w0_split, 3)
            pe.wait_ge(w1_in, 16)
            for s in range(LEAD):
                select(s)
            for s in range(LAST):
                bt, v = divmod(s, SPT)
                if s + LEAD < STEPS:
                    select(s + LEAD)
                if (i := chunk_at(s, TURN_A)) is not None:
                    turn_a(i)
                if bt + 1 < TILES and v in (X_AT, X_AT + 1):
                    turn_x(bt + 1, v - X_AT)
                if (i := chunk_at(s, TURN_XI)) is not None:
                    turn_xi(i)
                for r, at in enumerate(G_AT):
                    if (i := chunk_at(s, at)) is not None:
                        g_block(SUBS * i + r)
                tile, k = divmod(s - S2_AT, SPT)
                if 0 <= tile < TILES - 1 and k < S2_STEPS[tile]:
                    layer2(tile, F * k // S2_STEPS[tile], F * (k + 1) // S2_STEPS[tile])
                if (i := chunk_at(s, FILL_A)) is not None and (i + 1) % CPT:
                    fill_a(i + 1)
                if LAG <= s < STEPS + LAG:
                    layer1(s - LAG)
                if bt + 1 < TILES and v == A_AT:
                    fill_a(CPT * (bt + 1))
                if s >= MLP_AT and (s - MLP_AT) % 2 == 0 and (s - MLP_AT) // 2 < H1T + H2T:
                    k = (s - MLP_AT) // 2
                    if k == 0:
                        pe.wait_ge(mlp_in, 16 * 7)
                        pe.wait_ge(z_copied, 2 * (TILES - 1))
                    if k < H1T:
                        mlp1(0, k)
                    else:
                        mlp2(0, k - H1T)
            layer2(TILES - 1, 0, F)
            mlp3(0)
            pe.wait_ge(z_copied, 2 * TILES - 1)
            for k in range(3):
                mlp1(1, k, second=False)
            pe.wait_ge(z_copied, 2 * TILES)
            for k in range(3):
                mlp1(1, k, first=False)
            for k in range(3, H1T):
                mlp1(1, k)
            for k in range(H2T):
                mlp2(1, k)
            mlp3(1)


def _pairs():
    places = [(PT - 1) * len(range(n, P, F)) + (n < REST) for n in range(F)]
    owned = [{(n + k) % F for k in range((F + 1) // 2)} for n in range(F)]
    while True:
        over = [n for n in range(F) if len(owned[n]) > places[n]]
        if not over:
            break
        came, queue = {over[0]: None}, [over[0]]
        for n in queue:
            if len(owned[n]) < places[n]:
                break
            for m in sorted(owned[n]):
                if m not in came:
                    came[m] = n
                    queue.append(m)
        while came[n] is not None:
            owned[came[n]].remove(n)
            owned[n].add(came[n])
            n = came[n]
    pairs = np.full((PT, P, 2), -1)
    left = [sorted(o) for o in owned]
    for t in range(PT - 1):
        for p in range(P):
            pairs[t, p] = p % F, left[p % F].pop()
    for n in range(REST):
        m = left[n].pop()
        for at in REST_AT:
            pairs[PT - 1, at + n] = n, m
    assert not any(left)
    return pairs


def _selections(pairs):
    s = np.zeros((R, PT + 1, P), np.float32)
    for t in range(PT + 1):
        for p in range(P):
            m = pairs[t, p, 1] if t < PT else p % F
            if m >= 0:
                s[m::F, t, p] = 1.0
    return s


def kernel(**inputs):
    import concourse.bacc as bacc
    import ml_dtypes
    from concourse.bass_utils import run_bass_kernel_spmd

    a = {k: np.asarray(v) for k, v in inputs.items()}
    pairs = _pairs()
    w0 = a["L0_rec_W0"]
    w0_pair = np.zeros((PT, P, O), w0.dtype)
    w0_mirror = np.zeros((PT, P, O), w0.dtype)
    for t, p in zip(*np.nonzero(pairs[:, :, 1] >= 0)):
        n, m = pairs[t, p]
        w0_pair[t, p] = w0[n * F + m]
        if n != m:
            w0_mirror[t, p] = w0[m * F + n]
    arrays = {
        "ids": np.ascontiguousarray(a["ids"].reshape(TILES, P, F).transpose(1, 0, 2)),
        "dense_t": np.ascontiguousarray(a["dense_ctx"].T),
        "w0_pair": w0_pair,
        "w0_mirror": w0_mirror,
        "w1": a["L0_rec_W1"],
        "wt1": a["W_top1"],
        "bt1": np.ascontiguousarray(a["b_top1"].reshape(H1T, P).T),
        "wt2": a["W_top2"],
        "bt2": np.ascontiguousarray(a["b_top2"].reshape(H2T, P).T),
        "wt3": np.ascontiguousarray(a["W_top3"].reshape(H2T, P).T),
        "select": _selections(pairs).astype(ml_dtypes.bfloat16),
        "ident16": np.eye(P, dtype=ml_dtypes.bfloat16),
        "ident32": np.eye(P, dtype=np.float32),
    }
    arrays.update({f"tbl_{f}": a[f"tbl_{f}"] for f in range(F)})
    nc = bacc.Bacc("TRN2", target_bir_lowering=False, num_devices=1)
    aps = {k: nc.dram_tensor(k, v.shape, mybir.dt.from_np(v.dtype), kind="ExternalInput").ap()
           for k, v in arrays.items()}
    tables = [aps.pop(f"tbl_{f}") for f in range(F)]
    out = nc.dram_tensor("y", (B, 1), mybir.dt.float32, kind="ExternalOutput").ap()
    build(nc, tables=tables, out=out, **aps)
    return run_bass_kernel_spmd(nc, [arrays], core_ids=[0]).results[0]["y"]
```

```python
from contextlib import ExitStack

import concourse.bass as bass
import concourse.mybir as mybir
import numpy as np

F = 39
D = 16
B = 512
O = 128
P = 128
TILES = B // P
PARTS = 3
R = PARTS * F
PAIRS = F * (F + 1) // 2
PT = -(-PAIRS // P)
REST = PAIRS - (PT - 1) * P
REST_AT = (0, F, 2 * F)
REST_LO = 64
REST_ROWS = 96
ROWS = [P] * (PT - 1) + [REST_ROWS]
assert REST <= F and REST_AT[1] >= 32 and REST_AT[1] + REST <= REST_LO <= REST_AT[2] and REST_AT[2] + REST <= REST_ROWS
CH = 512
CB = CH // D
CPT = P // CB
CHUNKS = TILES * CPT
SUBS = CH // P
SB = P // D
GW = F + 1
STEPS = CHUNKS * PT
SPT = CPT * PT
LAG = 5
B_RING = 2
G_RING = 1
G_FIRST = False 
DIRECT = [[1, 4], [3], [], []]
Z_LAG = 2 
LEAD = 1
RING = LAG + 2
LOOK_P = 125
W0_AT = 2
TAIL0 = 6
CUTS = [13, 26]
CUTS1 = [18, 29]
W1_PIECES = 3 
LOOK_AGAIN = 6
LOOK_AT = 2
LOOK_LAG = 1
LOOK_N = 17
BATCH = 4
LOOK_MAX = 1250
COPY_XI = PT - 1 + LAG
TURN_XI = COPY_XI + 2
G_AT = [TURN_XI + 4 + 2 * r for r in range(CH // P)]
TURN_A = 1
REST_XI = TURN_XI + 1
REST_XT = TURN_A + 1 
FILL_A = 3
LAST = STEPS - PT + G_AT[-1] + 1
SPLIT_STEP = [1, 2, 3]
SPLIT_AT = [8, 14, 20]
X_AT = [24, 25]
TAKE_X = [24, 25]
A_AT = 26
S2_AT = SPT - PT + G_AT[-1] + 1
S2_STEPS = [SPT - 2] * (TILES - 2) + [12]
MLP_AT = S2_AT + SPT * (TILES - 2) + 15
HID1, HID2, DC = 512, 256, 16
H1T, H2T = HID1 // P, HID2 // P
XJ = 2


def direct(s):
    return s % PT in DIRECT[s // (CPT * PT)]


SPLITS = np.cumsum([0] + [not direct(s) for s in range(STEPS)]).tolist()

DIRECT_STEPS = [s for s in range(STEPS) if direct(s)]


def chunk_at(s, offset):
    i, rest = divmod(s - offset, PT)
    return i if rest == 0 and 0 <= i < CHUNKS else None


def build(nc, ids, ids_small, ids_again, row_numbers, tables, order, dense_t, w0_pair, w0_mirror, w1, wt1, bt1, wt2, bt2, wt3, select, ident16, ident32, out):
    f32, bf16, f32r, i32 = mybir.dt.float32, mybir.dt.bfloat16, mybir.dt.float32r, mybir.dt.int32
    ACT, ALU = mybir.ActivationFunctionType, mybir.AluOpType
    rows_of = [tables[f].shape[0] for f in order]
    small = min(LOOK_N, sum(n <= LOOK_MAX for n in rows_of))
    blocks_of = [n // LOOK_P for n in rows_of[:small]]
    most = max(blocks_of)
    half = F - TAIL0
    groups = [[(small, half), (half, F)]] + [[(0, CUTS[0]), (CUTS[0], CUTS[1]), (CUTS[1], F)]] * (TILES - 1)
    groups[1] = [(LOOK_AGAIN, CUTS1[0]), (CUTS1[0], CUTS1[1]), (CUTS1[1], F)]
    split_no = {}
    for bt in range(TILES):
        for k in range(len(groups[bt])):
            split_no[bt, k] = len(split_no)
    batches = []
    for n in range(small):
        if batches and blocks_of[n] == blocks_of[batches[-1][0]] and n - batches[-1][0] < BATCH:
            batches[-1] = (batches[-1][0], n + 1)
        else:
            batches.append((n, n + 1))
    LOOK_BANK = 512 // (PARTS * D)
    ctx = ExitStack()
    with ctx:
        def sb(name, shape, dt=f32):
            return ctx.enter_context(nc.sbuf_tensor(name, shape, dt))

        def bank(name):
            return ctx.enter_context(nc.psum_tensor(name, [P, 512], f32))

        def sem(name):
            return ctx.enter_context(nc.semaphore(name))

        ids_sb = sb("ids_sb", [P, TILES, F], i32)
        emb = sb("emb", [P, TILES, F * D])
        parts = sb("parts", [P, PARTS, F * D], bf16)
        xs = sb("xs", [R, 2, P, D], bf16)
        xa = sb("xa", [P, 2, P, D])
        sel = sb("sel", [R, PT + 1, P], bf16)
        id16 = sb("id16", [P, P], bf16)
        id32 = sb("id32", [P, P])
        z = sb("z", [P, Z_LAG + 2, CH])
        z_hi = sb("z_hi", [P, RING, CH], f32r)
        z_lo = sb("z_lo", [P, RING, CH], f32r)
        w0p = sb("w0p", [P, PT, O])
        w0m = sb("w0m", [P, PT, O])
        w0_hi = sb("w0_hi", [P, PT, O], f32r)
        w0_lo = sb("w0_lo", [P, PT, O], f32r)
        w0_rest = sb("w0_rest", [REST_ROWS, O], f32r)
        xi = sb("xi", [O, CH])
        xit_hi = sb("xit_hi", [P, 2, CH], f32r)
        xit_lo = sb("xit_lo", [P, 2, CH], f32r)
        xt = sb("xt", [P, 2, 2, SUBS, GW], f32r)
        diag = sb("diag", [P, 2, 2, SUBS, SB, GW], f32r)
        g = sb("g", [O, 2, GW, P])
        w1_sb = sb("w1_sb", [O, F, O])
        z1 = sb("z1", [O, B])
        z2 = sb("z2", [O, B])
        dt_sb = sb("dt_sb", [DC, B])
        whole = [z1, z2]
        wt1_sb = sb("wt1_sb", [P, 2, HID1])
        wt1c_sb = sb("wt1c_sb", [DC, HID1])
        wt2_sb = sb("wt2_sb", [P, H1T, HID2])
        wt3_sb = sb("wt3_sb", [P, H2T])
        bt1_sb = sb("bt1_sb", [P, H1T])
        bt2_sb = sb("bt2_sb", [P, H2T])
        hidden = g[:, 0, :, :].rearrange("p m b -> p (m b)")
        h1 = hidden[:, 0:H1T * B].rearrange("p (k b) -> p k b", b=B)
        h2 = hidden[:, H1T * B:(H1T + H2T) * B].rearrange("p (k b) -> p k b", b=B)
        y_sb = sb("y_sb", [1, B])

        g_mem = g[0:LOOK_P, :, :, :].rearrange("p s m b -> p (s m b)")
        w1_mem = w1_sb[0:LOOK_P, :, :].rearrange("p m o -> p (m o)")
        used = 0
        table = g_mem[:, used:used + small * most * D].rearrange("p (n c d) -> p n c d", n=small, d=D)
        used += small * most * D
        size = small * most * PARTS * D // 2
        table_parts = g_mem[:, used:used + size].bitcast(bf16).rearrange("p (n c k d) -> p n c k d", n=small, c=most, d=D)
        used += size
        ids_row = g_mem[:, used:used + small * P].bitcast(i32)
        used = small * P // 2
        ids16 = w1_mem[:, 0:used].bitcast(mybir.dt.int16)
        size = most * P // 2
        ids16_again = w1_mem[:, used:used + LOOK_AGAIN * P // 2].bitcast(mybir.dt.int16)
        used += LOOK_AGAIN * P // 2
        ids_row_again = z[0:LOOK_P, :, :].rearrange("p k c -> p (k c)")[:, 0:LOOK_AGAIN * P].bitcast(i32)
        numbers, start = {}, used
        for c in sorted(set(blocks_of)):
            numbers[c] = w1_mem[:, start:start + c * P // 2].bitcast(mybir.dt.int16)
            start += c * P // 2
        all_numbers = w1_mem[:, used:start].bitcast(mybir.dt.int16)
        one_hot = []
        for j in range(3):
            one_hot.append(w1_mem[:, start:start + size].bitcast(bf16).rearrange("p (c b) -> p c b", b=P))
            start += size

        b_bank = [bank(f"b_bank{j}") for j in range(B_RING)]
        l1_bank = [bank(f"l1_bank{j}") for j in range(2)]
        turn_bank = bank("turn_bank")
        xi_bank = bank("xi_bank")
        g_bank = [bank(f"g_bank{j}") for j in range(G_RING)]
        s2_bank = bank("s2_bank")
        turn_banks = [turn_bank, xi_bank, g_bank[0]]

        ids_in = sem("ids_in")
        consts_in = sem("consts_in")
        w0_in = sem("w0_in")
        w1_in = sem("w1_in")
        mlp_in = sem("mlp_in")
        gathered = {key: sem(f"gathered{key[0]}_{key[1]}") for key in split_no}
        look_in = sem("look_in")
        again_in = sem("again_in")
        table_in = [sem(f"table_in{k}") for k in range(len(batches))]
        table_hi = sem("table_hi")
        table_rest = sem("table_rest")
        table_mid = sem("table_mid")
        table_lo = sem("table_lo")
        ids_cast = sem("ids_cast")
        matched = sem("matched")
        looked_up = sem("looked_up")
        look_copied = sem("look_copied")
        zero_src = sem("zero_src")
        hi_cast = sem("hi_cast")
        rest1 = sem("rest1")
        mid_cast = sem("mid_cast")
        lo_cast = sem("lo_cast")
        turn_filled = [sem(f"turn_filled{k}") for k in range(3)]
        turn_taken = [sem(f"turn_taken{k}") for k in range(3)]
        chunk0_taken = sem("chunk0_taken")
        xt_hi_done = sem("xt_hi_done")
        w0_summed = sem("w0_summed")
        w0_rounded = sem("w0_rounded")
        w0_split = sem("w0_split")
        zeroed = sem("zeroed")
        ones_set = sem("ones_set")
        selected = sem("selected")
        product = sem("product")
        rounded = sem("rounded")
        remainder = sem("remainder")
        l1_used = sem("l1_used")
        xi_copied = sem("xi_copied")
        xit_hi_done = sem("xit_hi_done")
        diag_in = [sem(f"diag_in{j}") for j in range(2)]
        g_summed = sem("g_summed")
        g_copied = sem("g_copied")
        s2_done = sem("s2_done")
        z_copied = sem("z_copied")
        mlp_mm = sem("mlp_mm")
        mlp_act = sem("mlp_act")
        y_copied = sem("y_copied")
        y_out = sem("y_out")

        block = ctx.enter_context(nc.Block())

        fills = [[("x", 0, 0)], [("x", 0, 1)], [("a", 0, 0)]]
        for s in range(LAST):
            bt, v = divmod(s, SPT)
            if (i := chunk_at(s, TURN_A)) is not None:
                fills[0].append(("xt", i, 0))
            for k, at in enumerate(X_AT):
                if bt + 1 < TILES and v == at:
                    fills[k].append(("x", bt + 1, k))
            if (i := chunk_at(s, TURN_XI)) is not None:
                fills[1].append(("xi", i, 0))
            if (i := chunk_at(s, FILL_A)) is not None and (i + 1) % CPT:
                fills[0].append(("a", i + 1, 0))
            if bt + 1 < TILES and v == A_AT:
                fills[0].append(("a", CPT * (bt + 1), 0))
        fill = {job: (k, n) for k, jobs in enumerate(fills) for n, job in enumerate(jobs)}

        def after(sems, *job):
            k, n = fill[job]
            return sems[k], n + 1

        GATE = [0, 3 * P, B]
        MLP_MM = H1T + H2T + 1
        mlp_bank = [*b_bank, l1_bank[0], s2_bank, *b_bank]

        @block.gpsimd
        def _(pool):
            pool.wait_ge(ids_in, 16)
            for bt in range(TILES):
                for k, (lo, hi) in enumerate(groups[bt]):
                    for n in range(lo, hi):
                        nc.gpsimd.indirect_dma_start(
                            emb[:, bt, n * D:(n + 1) * D], None, tables[order[n]],
                            bass.IndirectOffsetOnAxis(ids_sb[:, bt, order[n]:order[n] + 1], 0)
                        ).then_inc(gathered[bt, k], 16)

        @block.sync
        def _(sp):
            sp.dma_start(ids_sb[:], ids).then_inc(ids_in, 16)
            sp.dma_start(ids_row, ids_small.rearrange("n b -> (n b)").unsqueeze(0).broadcast_to([LOOK_P, small * P])).then_inc(look_in, 16)
            sp.dma_start(all_numbers, row_numbers).then_inc(look_in, 16)
            for k, (lo, hi) in enumerate(batches):
                for n in range(lo, hi):
                    sp.dma_start(table[:, n, 0:blocks_of[n], :],
                                 tables[order[n]].rearrange("(p c) d -> p c d", p=LOOK_P)).then_inc(table_in[k], 16)
            sp.dma_start(ids_row_again, ids_again.rearrange("n b -> (n b)").unsqueeze(0).broadcast_to([LOOK_P, LOOK_AGAIN * P])).then_inc(again_in, 16)
            sp.dma_start(sel[:], select).then_inc(consts_in, 16)
            sp.dma_start(id16[:], ident16).then_inc(consts_in, 16)
            sp.dma_start(id32[:], ident32).then_inc(consts_in, 16)
            sp.dma_start(w0p[:], w0_pair.rearrange("t p o -> p t o")).then_inc(w0_in, 16)
            sp.dma_start(w0m[:], w0_mirror.rearrange("t p o -> p t o")).then_inc(w0_in, 16)
            sp.wait_ge(zero_src, 1)
            sp.dma_start(diag[:].rearrange("p i h s b m -> p (i h s) (b m)").bitcast(f32),
                         z1[:, 0:SB * GW].unsqueeze(1).broadcast_to([P, 4 * SUBS, SB * GW])).then_inc(zeroed, 16)
            sp.dma_start(wt1_sb[:], wt1[0:2 * P, :].rearrange("(k p) h -> p k h", p=P)).then_inc(mlp_in, 16)
            sp.dma_start(wt1c_sb[:], wt1[2 * P:2 * P + DC, :]).then_inc(mlp_in, 16)
            sp.dma_start(wt2_sb[:], wt2.rearrange("(k p) h -> p k h", p=P)).then_inc(mlp_in, 16)
            sp.dma_start(wt3_sb[:], wt3).then_inc(mlp_in, 16)
            sp.dma_start(bt1_sb[:], bt1).then_inc(mlp_in, 16)
            sp.dma_start(bt2_sb[:], bt2).then_inc(mlp_in, 16)
            sp.dma_start(dt_sb[:], dense_t).then_inc(mlp_in, 16)
            sp.wait_ge(zeroed, 16)
            sp.wait_ge(ones_set, 2)
            for i in range(CHUNKS):
                sp.wait_ge(*after(turn_taken, "xt", i, 0))
                if i >= 2:
                    sp.wait_ge(g_summed, SUBS * (i - 1))
                for b in range(SB):
                    sp.dma_start(diag[b * D:(b + 1) * D, i % 2, :, :, b, :].bitcast(f32),
                                 xt[b * D:(b + 1) * D, i % 2, :, :, :].bitcast(f32)).then_inc(diag_in[i % 2], 16)
                if i < W1_PIECES:
                    if i == 0:
                        sp.wait_ge(looked_up, small + LOOK_AGAIN)
                    m = slice(i * F // W1_PIECES, (i + 1) * F // W1_PIECES)
                    sp.dma_start(w1_sb[:, m, :], w1.rearrange("(m n) o -> n m o", n=O)[:, m, :]).then_inc(w1_in, 16)
            sp.wait_ge(y_copied, 2)
            sp.dma_start(out.rearrange("b o -> o b"), y_sb[:]).then_inc(y_out, 16)
            sp.wait_ge(y_out, 16)

        @block.scalar
        def _(act):
            def cast_hi(bt, k):
                lo, hi = (n * D for n in groups[bt][k])
                act.wait_ge(gathered[bt, k], hi - lo)
                if bt:
                    act.wait_ge(*after(turn_filled, "x", bt - 1, XJ - 1))
                nc.scalar.activation(parts[:, 0, lo:hi], emb[:, bt, lo:hi], ACT.Copy).then_inc(hi_cast, 1)

            def cast_mid(bt, k):
                lo, hi = (n * D for n in groups[bt][k])
                act.wait_ge(rest1, split_no[bt, k] + 1)
                nc.scalar.activation(parts[:, 1, lo:hi], emb[:, bt, lo:hi], ACT.Copy).then_inc(mid_cast, 1)

            def take_x(bt, k, first=0, signal=None):
                end = CB if signal else P
                act.wait_ge(*after(turn_filled, "x", bt, k))
                nc.scalar.activation(
                    xs[:, bt % 2, first:end, k * D // XJ:(k + 1) * D // XJ],
                    turn_banks[k][0:R, :].bitcast(bf16).rearrange("p (d b) -> p b d", b=P)[:, first:end, :],
                    ACT.Copy).then_inc(signal or turn_taken[k], 1)

            def take_a(i):
                bt, c = divmod(i, CPT)
                act.wait_ge(*after(turn_filled, "a", i, 0))
                k = fill["a", i, 0][0]
                nc.scalar.activation(xa[:, bt % 2, c * CB:(c + 1) * CB, :],
                                     turn_banks[k][:].rearrange("p (b d) -> p b d", d=D),
                                     ACT.Copy).then_inc(turn_taken[k], 1)

            def take_xt(i):
                act.wait_ge(*after(turn_filled, "xt", i, 0))
                if i >= 2:
                    act.wait_ge(diag_in[i % 2], 16 * SB * (i // 2))
                nc.scalar.activation(xt[:, i % 2, 0, :, 0:F],
                                     turn_bank[:, 0:SUBS * GW].rearrange("p (s m) -> p s m", m=GW)[:, :, 0:F],
                                     ACT.Copy).then_inc(xt_hi_done, 1)

            def table_cast(part, k, after):
                lo, hi = batches[k]
                c = blocks_of[lo]
                nc.scalar.activation(table_parts[:, lo:hi, 0:c, part, :], table[:, lo:hi, 0:c, :],
                                     ACT.Copy).then_inc(after, 1)

            act.wait_ge(look_in, 32)
            nc.scalar.activation(ids16, ids_row, ACT.Copy).then_inc(ids_cast, 1)
            for k in range(len(batches) + 1):
                if k < len(batches):
                    act.wait_ge(table_in[k], 16 * (batches[k][1] - batches[k][0]))
                    table_cast(0, k, table_hi)
                if k:
                    act.wait_ge(table_rest, k)
                    table_cast(1, k - 1, table_mid)

            act.wait_ge(again_in, 16)
            nc.scalar.activation(ids16_again, ids_row_again, ACT.Copy).then_inc(ids_cast, 1)

            def take_looked_up_again():
                act.wait_ge(looked_up, small + LOOK_AGAIN)
                for k in range(XJ):
                    act.wait_ge(*after(turn_filled, "x", 0, k))
                nc.scalar.activation(
                    parts[:, :, 0:LOOK_AGAIN * D].rearrange("p k (n d) -> p n k d", d=D),
                    g_bank[0][:, 0:LOOK_AGAIN * PARTS * D].rearrange("p (n k d) -> p n k d", k=PARTS, d=D),
                    ACT.Copy).then_inc(look_copied, 1)

            def take_looked_up(lo, hi):
                act.wait_ge(looked_up, hi)
                nc.scalar.activation(
                    parts[:, :, lo * D:hi * D].rearrange("p k (n d) -> p n k d", d=D),
                    b_bank[lo // LOOK_BANK][:, 0:(hi - lo) * PARTS * D].rearrange("p (n k d) -> p n k d", k=PARTS, d=D),
                    ACT.Copy).then_inc(look_copied, 1)

            cast_hi(0, 0)
            cast_mid(0, 0)
            for lo in range(0, small, LOOK_BANK):
                take_looked_up(lo, min(small, lo + LOOK_BANK))
            cast_hi(0, 1)
            cast_mid(0, 1)
            act.wait_ge(w0_summed, 1)
            nc.scalar.activation(w0_hi[:], w0p[:], ACT.Copy).then_inc(w0_rounded, 1)
            take_x(0, 0, signal=chunk0_taken)
            take_a(0)
            take_x(0, 0, first=CB)

            def round_z(s):
                rows = ROWS[s % PT]
                if direct(s):
                    return
                at = SPLITS[s] % (Z_LAG + 2)
                act.wait_ge(product, s + 1)
                if s >= RING:
                    act.wait_ge(l1_used, s - RING + 1)
                nc.scalar.activation(z_hi[0:rows, s % RING, :], z[0:rows, at, :], ACT.Copy).then_inc(rounded, 1)

            def take_g(j):
                bt, block = divmod(j, CPT * SUBS)
                act.wait_ge(g_summed, j + 1)
                if bt >= 2 and block == 0:
                    act.wait_ge(s2_done, bt - 1)
                    act.wait_ge(z_copied, 2 * (bt - 1))
                nc.scalar.activation(g[:, bt % 2, :, block * SB:(block + 1) * SB],
                                     g_bank[j % G_RING][:, 0:SB * GW].rearrange("p (b m) -> p m b", m=GW),
                                     ACT.Copy).then_inc(g_copied, 1)

            def take_xi(i):
                act.wait_ge(l1_used, PT * (i + 1))
                if i:
                    act.wait_ge(*after(turn_filled, "xi", i - 1, 0))
                nc.scalar.activation(xi[:], l1_bank[i % 2][:], ACT.Copy).then_inc(xi_copied, 1)

            def round_xit(i):
                act.wait_ge(*after(turn_filled, "xi", i, 0))
                if i >= 2:
                    act.wait_ge(g_summed, SUBS * (i - 1))
                nc.scalar.activation(xit_hi[:, i % 2, :], xi_bank[:], ACT.Copy).then_inc(xit_hi_done, 1)

            def relu(m, k):
                lo, hi = GATE[m:m + 2]
                if m == 0 and k == 0:
                    act.wait_ge(mlp_in, 16 * 7)
                    act.wait_ge(s2_done, TILES - 1)
                act.wait_ge(mlp_mm, MLP_MM * m + k + 1)
                h, bias, j = (h1, bt1_sb, k) if k < H1T else (h2, bt2_sb, k - H1T)
                nc.scalar.activation(h[:, j, lo:hi], mlp_bank[k][:, 0:hi - lo], ACT.Relu,
                                     bias=bias[:, j:j + 1]).then_inc(mlp_act, 1)

            for s in range(LAST):
                bt, v = divmod(s, SPT)
                if s == LOOK_AT + LOOK_AGAIN + LOOK_LAG:
                    take_looked_up_again()
                if G_FIRST:
                    for r, at in enumerate(G_AT):
                        if (i := chunk_at(s, at)) is not None:
                            take_g(SUBS * i + r)
                if s < STEPS:
                    round_z(s)
                if not G_FIRST:
                    for r, at in enumerate(G_AT):
                        if (i := chunk_at(s, at)) is not None:
                            take_g(SUBS * i + r)
                if (i := chunk_at(s, COPY_XI)) is not None:
                    take_xi(i)
                if (i := chunk_at(s, TURN_XI)) is not None:
                    round_xit(i)
                if (i := chunk_at(s, TURN_A)) is not None:
                    take_xt(i)
                if (i := chunk_at(s, FILL_A)) is not None and (i + 1) % CPT:
                    take_a(i + 1)
                if bt + 1 < TILES:
                    for k, at in enumerate(SPLIT_AT):
                        if v == at:
                            cast_hi(bt + 1, k)
                        if v == at + SPLIT_STEP[1]:
                            cast_mid(bt + 1, k)
                    for k, at in enumerate(TAKE_X):
                        if v == at:
                            take_x(bt + 1, k)
                    if v == A_AT:
                        take_a(CPT * (bt + 1))
                if s >= MLP_AT and (s - MLP_AT) % 2 == 0 and (s - MLP_AT) // 2 < H1T + H2T:
                    relu(0, (s - MLP_AT) // 2)

            for k in range(H1T + H2T):
                relu(1, k)

        @block.vector
        def _(dve):
            def rest_hi(bt, k):
                lo, hi = (n * D for n in groups[bt][k])
                dve.wait_ge(hi_cast, split_no[bt, k] + 1)
                nc.vector.tensor_sub(emb[:, bt, lo:hi], emb[:, bt, lo:hi], parts[:, 0, lo:hi]).then_inc(rest1, 1)

            def rest_mid(bt, k):
                lo, hi = (n * D for n in groups[bt][k])
                dve.wait_ge(mid_cast, split_no[bt, k] + 1)
                if bt:
                    dve.wait_ge(*after(turn_filled, "x", bt - 1, XJ - 1))
                nc.vector.tensor_sub(parts[:, 2, lo:hi], emb[:, bt, lo:hi], parts[:, 1, lo:hi]).then_inc(lo_cast, 1)

            nc.vector.memset(z1[:, 0:SB * GW], 0.0).then_inc(zero_src, 1)
            nc.vector.memset(xt[:, :, 0, :, F:GW].bitcast(f32), 1.0).then_inc(ones_set, 1)
            nc.vector.memset(xt[:, :, 1, :, F:GW].bitcast(f32), 0.0).then_inc(ones_set, 1)

            def match(n, again=False):
                c = blocks_of[n]
                number = small + n if again else n
                if number >= 3:
                    dve.wait_ge(looked_up, number - 2)
                nc.vector.tensor_tensor(
                    one_hot[number % 3][:, 0:c, :],
                    (ids16_again if again else ids16)[:, n * P:(n + 1) * P].unsqueeze(1).broadcast_to([LOOK_P, c, P]),
                    numbers[c].rearrange("p (c b) -> p c b", b=P), ALU.is_equal).then_inc(matched, 1)

            def first_rest(k):
                lo, hi = batches[k]
                c = blocks_of[lo]
                dve.wait_ge(table_hi, k + 1)
                nc.vector.tensor_sub(table[:, lo:hi, 0:c, :], table[:, lo:hi, 0:c, :],
                                     table_parts[:, lo:hi, 0:c, 0, :]).then_inc(table_rest, 1)

            def last_rest(k):
                lo, hi = batches[k]
                c = blocks_of[lo]
                dve.wait_ge(table_mid, k + 1)
                nc.vector.tensor_sub(table_parts[:, lo:hi, 0:c, 2, :], table[:, lo:hi, 0:c, :],
                                     table_parts[:, lo:hi, 0:c, 1, :]).then_inc(table_lo, 1)

            dve.wait_ge(look_in, 32)
            dve.wait_ge(ids_cast, 1)
            for k in range(len(batches)):
                if k == 0:
                    first_rest(0)
                    for n in range(3):
                        match(n)
                    last_rest(0)
                    if len(batches) > 1:
                        first_rest(1)
                for n in range(max(3, batches[k][0]), batches[k][1]):
                    match(n)
                if k + 1 < len(batches):
                    last_rest(k + 1)
                if k + 2 < len(batches):
                    first_rest(k + 2)
            for k in range(len(groups[0])):
                rest_hi(0, k)
                rest_mid(0, k)
            dve.wait_ge(w0_in, 32)
            nc.vector.tensor_add(w0p[:], w0p[:], w0m[:]).then_inc(w0_summed, 1)
            def take_x(first, end, signal):
                dve.wait_ge(*after(turn_filled, "x", 0, 1))
                nc.vector.tensor_copy(
                    xs[:, 0, first:end, D // XJ:D],
                    turn_banks[1][0:R, :].bitcast(bf16).rearrange("p (d b) -> p b d", b=P)[:, first:end, :]
                ).then_inc(signal, 1)

            take_x(0, CB, chunk0_taken)

            def split_w0():
                dve.wait_ge(w0_rounded, 1)
                nc.vector.tensor_sub(w0_lo[:], w0p[:], w0_hi[:].bitcast(f32)).then_inc(w0_summed, 1)
                dve.wait_ge(w0_summed, 2)
                for lo in range(0, REST_ROWS, 32):
                    w = w0_lo if lo == 32 else w0_hi
                    nc.vector.tensor_copy(w0_rest[lo:lo + 32, :], w[lo:lo + 32, PT - 1, :]).then_inc(w0_split, 1)

            dve.wait_ge(ids_cast, 2)

            def multiply(s):
                i, t = divmod(s, PT)
                bt, c = divmod(i, CPT)
                rows = ROWS[t]
                if direct(s):
                    number = s - SPLITS[s]
                    if number == 0:
                        dve.wait_ge(zeroed, 16)
                    if number >= 2:
                        dve.wait_ge(l1_used, DIRECT_STEPS[number - 2] + 1)
                    target = whole[number % 2][0:rows, :]
                else:
                    if SPLITS[s] >= Z_LAG + 2:
                        dve.wait_ge(remainder, SPLITS[s] - Z_LAG - 1)
                        dve.wait_ge(rounded, SPLITS[s] - Z_LAG - 1)
                    target = z[0:rows, SPLITS[s] % (Z_LAG + 2), :]
                if t == 0:
                    dve.wait_ge(*after(turn_taken, "a", i, 0))
                dve.wait_ge(selected, s + 1)
                nc.vector.tensor_tensor(target,
                                        xa[0:rows, bt % 2, c * CB:(c + 1) * CB, :].rearrange("p b d -> p (b d)"),
                                        b_bank[s % B_RING][0:rows, :], ALU.mult).then_inc(product, 1)

            def rest_z(s):
                if direct(s):
                    return
                rows = ROWS[s % PT]
                dve.wait_ge(rounded, SPLITS[s] + 1)
                if s >= RING:
                    dve.wait_ge(l1_used, s - RING + 1)
                low = z_lo if s % PT < PT - 1 else z_hi
                first = 0 if s % PT < PT - 1 else REST_LO
                nc.vector.tensor_sub(low[first:rows, s % RING, :], z[first:rows, SPLITS[s] % (Z_LAG + 2), :],
                                     z_hi[first:rows, s % RING, :].bitcast(f32)).then_inc(remainder, 1)

            def rest_xit(i):
                dve.wait_ge(xit_hi_done, i + 1)
                if i >= 2:
                    dve.wait_ge(g_summed, SUBS * (i - 1))
                nc.vector.tensor_sub(xit_lo[:, i % 2, :], xi_bank[:],
                                     xit_hi[:, i % 2, :].bitcast(f32)).then_inc(turn_taken[1], 1)

            def rest_xt(i):
                dve.wait_ge(xt_hi_done, i + 1)
                if i >= 2:
                    dve.wait_ge(diag_in[i % 2], 16 * SB * (i // 2))
                nc.vector.tensor_sub(xt[:, i % 2, 1, :, 0:F],
                                     turn_bank[:, 0:SUBS * GW].rearrange("p (s m) -> p s m", m=GW)[:, :, 0:F],
                                     xt[:, i % 2, 0, :, 0:F].bitcast(f32)).then_inc(turn_taken[0], 1)

            def copy_z(bt):
                cols = slice(bt * P, (bt + 1) * P)
                dve.wait_ge(g_copied, CPT * SUBS * (bt + 1))
                nc.vector.tensor_copy(z1[:, cols], g[:, bt % 2, F, :]).then_inc(z_copied, 1)
                dve.wait_ge(s2_done, bt + 1)
                nc.vector.tensor_copy(z2[:, cols], s2_bank[:, 0:P]).then_inc(z_copied, 1)

            for s in range(LAST):
                bt, v = divmod(s, SPT)
                if s < STEPS:
                    multiply(s)
                if s == 0:
                    take_x(CB, P, turn_taken[1])
                if 0 <= s - LOOK_AT < LOOK_AGAIN:
                    match(s - LOOK_AT, again=True)
                if s == W0_AT:
                    split_w0()
                if Z_LAG <= s < STEPS + Z_LAG:
                    rest_z(s - Z_LAG)
                if (i := chunk_at(s, REST_XI)) is not None:
                    rest_xit(i)
                if (i := chunk_at(s, REST_XT)) is not None:
                    rest_xt(i)
                if bt + 1 < TILES:
                    for k, at in enumerate(SPLIT_AT):
                        if v == at + SPLIT_STEP[0]:
                            rest_hi(bt + 1, k)
                        if v == at + SPLIT_STEP[2]:
                            rest_mid(bt + 1, k)
                tile, k = divmod(s - S2_AT, SPT)
                if 0 <= tile < TILES - 1 and k == S2_STEPS[tile]:
                    copy_z(tile)
            copy_z(TILES - 1)
            for m in range(2):
                lo, hi = GATE[m:m + 2]
                dve.wait_ge(mlp_mm, MLP_MM * (m + 1))
                nc.vector.tensor_copy(y_sb[:, lo:hi], l1_bank[1][0:1, lo:hi]).then_inc(y_copied, 1)

        @block.tensor
        def _(pe):
            def turn_free(*job):
                k, n = fill[job]
                if n:
                    pe.wait_ge(turn_taken[k], n)

            def turn_x(bt, k):
                turn_free("x", bt, k)
                if k == 0:
                    pe.wait_ge(lo_cast, split_no[bt, len(groups[bt]) - 1] + 1)
                    pe.wait_ge(look_copied, -(-small // LOOK_BANK) + (bt > 0))
                bank16 = turn_banks[k][:, :].bitcast(bf16)
                for j in range(D // XJ):
                    last = nc.tensor.transpose(bank16[0:R, j * P:(j + 1) * P],
                                               parts[:, :, :].rearrange("p k (m d) -> p (k m) d", d=D)[:, :, k * D // XJ + j],
                                               id16[:])
                last.then_inc(turn_filled[fill["x", bt, k][0]], 1)

            def features_there(i):
                bt, c = divmod(i, CPT)
                if i == 0:
                    pe.wait_ge(chunk0_taken, XJ)
                elif c == 0 or i == 1:
                    for k in range(XJ):
                        pe.wait_ge(*after(turn_taken, "x", bt, k))

            def columns(bt, c):
                return xs[:, bt % 2, c * CB:(c + 1) * CB, :].rearrange("p b d -> p (b d)")

            def fill_a(i):
                turn_free("a", i, 0)
                features_there(i)
                k = fill["a", i, 0][0]
                nc.tensor.matmul(turn_banks[k][:], sel[:, PT, :], columns(i // CPT, i % CPT),
                                 start=True, stop=True).then_inc(turn_filled[k], 1)

            def turn_a(i):
                bt, c = divmod(i, CPT)
                turn_free("xt", i, 0)
                for r in range(SUBS):
                    b0 = c * CB + r * SB
                    last = nc.tensor.transpose(turn_bank[:, r * GW:(r + 1) * GW],
                                               xa[0:GW, bt % 2, b0:b0 + SB, :].rearrange("p b d -> p (b d)"),
                                               id32[0:GW, 0:GW])
                last.then_inc(turn_filled[fill["xt", i, 0][0]], 1)

            def select(s):
                i, t = divmod(s, PT)
                bt, c = divmod(i, CPT)
                if s >= B_RING:
                    pe.wait_ge(product, s - B_RING + 1)
                if t == 0:
                    features_there(i)
                nc.tensor.matmul(b_bank[s % B_RING][0:ROWS[t], :], sel[:, t, 0:ROWS[t]], columns(bt, c),
                                 start=True, stop=True).then_inc(selected, 1)

            def layer1(s):
                i, t = divmod(s, PT)
                bank, slot = l1_bank[i % 2], s % RING
                if s == 0:
                    pe.wait_ge(w0_split, 3)
                if direct(s):
                    pe.wait_ge(product, s + 1)
                else:
                    pe.wait_ge(remainder, SPLITS[s] + 1)
                if t == 0 and i >= 2:
                    pe.wait_ge(xi_copied, i - 1)
                if direct(s):
                    nc.tensor.matmul(bank[:], w0p[:, t, :], whole[(s - SPLITS[s]) % 2][:],
                                     start=t == 0, stop=False).then_inc(l1_used, 1)
                elif t == PT - 1:
                    nc.tensor.matmul(bank[:], w0_rest[:], z_hi[0:REST_ROWS, slot, :],
                                     start=False, stop=True).then_inc(l1_used, 1)
                else:
                    nc.tensor.matmul(bank[:], w0_hi[:, t, :], z_hi[:, slot, :], start=t == 0, stop=False)
                    nc.tensor.matmul(bank[:], w0_hi[:, t, :], z_lo[:, slot, :], start=False, stop=False)
                    nc.tensor.matmul(bank[:], w0_lo[:, t, :], z_hi[:, slot, :],
                                     start=False, stop=False).then_inc(l1_used, 1)

            def turn_xi(i):
                pe.wait_ge(xi_copied, i + 1)
                turn_free("xi", i, 0)
                for r in range(SUBS):
                    last = nc.tensor.transpose(xi_bank[:, r * P:(r + 1) * P], xi[:, r * P:(r + 1) * P], id32[:])
                last.then_inc(turn_filled[fill["xi", i, 0][0]], 1)

            def g_block(j):
                i, r = divmod(j, SUBS)
                if r == 0:
                    pe.wait_ge(*after(turn_taken, "xi", i, 0))
                    pe.wait_ge(diag_in[i % 2], 16 * SB * (i // 2 + 1))
                if j >= G_RING:
                    pe.wait_ge(g_copied, j - G_RING + 1)
                x_hi, x_lo = (diag[:, i % 2, h, r, :, :].rearrange("p b m -> p (b m)") for h in range(2))
                y_hi, y_lo = (w[:, i % 2, r * P:(r + 1) * P] for w in (xit_hi, xit_lo))
                o = g_bank[j % G_RING][:, 0:SB * GW]
                nc.tensor.matmul(o, y_hi, x_hi, start=True, stop=False)
                nc.tensor.matmul(o, y_hi, x_lo, start=False, stop=False)
                nc.tensor.matmul(o, y_lo, x_hi, start=False, stop=True).then_inc(g_summed, 1)

            def layer2(bt, first, end):
                if first == end:
                    return
                if first == 0:
                    if bt == 0:
                        pe.wait_ge(w1_in, 16 * W1_PIECES)
                    pe.wait_ge(g_copied, CPT * SUBS * (bt + 1))
                    if bt:
                        pe.wait_ge(z_copied, 2 * bt)
                for m in range(first, end):
                    last = nc.tensor.matmul(s2_bank[:, 0:P], w1_sb[:, order[m], :], g[:, bt % 2, m, :],
                                            start=m == 0, stop=m == F - 1)
                if end == F:
                    last.then_inc(s2_done, 1)

            def mlp1(m, k, first=True, second=True):
                lo, hi = GATE[m:m + 2]
                o = mlp_bank[k][:, 0:hi - lo]
                h = slice(k * P, (k + 1) * P)
                if first:
                    if m:
                        pe.wait_ge(mlp_act, (H1T + H2T))
                    nc.tensor.matmul(o, wt1c_sb[:, h], dt_sb[:, lo:hi], start=True, stop=False)
                    nc.tensor.matmul(o, wt1_sb[:, 0, h], z1[:, lo:hi], start=False, stop=False)
                if second:
                    nc.tensor.matmul(o, wt1_sb[:, 1, h], z2[:, lo:hi], start=False, stop=True).then_inc(mlp_mm, 1)

            def mlp2(m, k):
                lo, hi = GATE[m:m + 2]
                pe.wait_ge(mlp_act, (H1T + H2T) * m + H1T)
                for kk in range(H1T):
                    last = nc.tensor.matmul(mlp_bank[H1T + k][:, 0:hi - lo], wt2_sb[:, kk, k * P:(k + 1) * P],
                                            h1[:, kk, lo:hi], start=kk == 0, stop=kk == H1T - 1)
                last.then_inc(mlp_mm, 1)

            def mlp3(m):
                lo, hi = GATE[m:m + 2]
                pe.wait_ge(mlp_act, (H1T + H2T) * (m + 1))
                if m:
                    pe.wait_ge(y_copied, 1)
                for k in range(H2T):
                    last = nc.tensor.matmul(l1_bank[1][0:1, lo:hi], wt3_sb[:, k:k + 1], h2[:, k, lo:hi],
                                            start=k == 0, stop=k == H2T - 1)
                last.then_inc(mlp_mm, 1)

            def look_up(n, again=False):
                number = small + n if again else n
                pe.wait_ge(matched, number + 1)
                bank, n0 = (g_bank[0], 0) if again else (b_bank[n // LOOK_BANK], n // LOOK_BANK * LOOK_BANK)
                at = (n - n0) * PARTS * D
                for c in range(blocks_of[n]):
                    last = nc.tensor.matmul(bank[:, at:at + PARTS * D], one_hot[number % 3][:, c, :],
                                            table_parts[:, n, c, :, :].rearrange("p k d -> p (k d)"),
                                            start=c == 0, stop=c == blocks_of[n] - 1)
                last.then_inc(looked_up, 1)

            for k, (lo, hi) in enumerate(batches):
                pe.wait_ge(table_lo, k + 1)
                for n in range(lo, hi):
                    look_up(n)
            pe.wait_ge(consts_in, 48)
            for k in range(XJ):
                turn_x(0, k)
            fill_a(0)
            for s in range(LEAD):
                select(s)
            for s in range(LAST):
                bt, v = divmod(s, SPT)
                if s + LEAD < STEPS:
                    select(s + LEAD)
                if 0 <= s - LOOK_AT - LOOK_LAG < LOOK_AGAIN:
                    look_up(s - LOOK_AT - LOOK_LAG, again=True)
                if (i := chunk_at(s, TURN_A)) is not None:
                    turn_a(i)
                for k, at in enumerate(X_AT):
                    if bt + 1 < TILES and v == at:
                        turn_x(bt + 1, k)
                if (i := chunk_at(s, TURN_XI)) is not None:
                    turn_xi(i)
                for r, at in enumerate(G_AT):
                    if (i := chunk_at(s, at)) is not None:
                        g_block(SUBS * i + r)
                tile, k = divmod(s - S2_AT, SPT)
                if 0 <= tile < TILES - 1 and k < S2_STEPS[tile]:
                    layer2(tile, F * k // S2_STEPS[tile], F * (k + 1) // S2_STEPS[tile])
                if (i := chunk_at(s, FILL_A)) is not None and (i + 1) % CPT:
                    fill_a(i + 1)
                if LAG <= s < STEPS + LAG:
                    layer1(s - LAG)
                if bt + 1 < TILES and v == A_AT:
                    fill_a(CPT * (bt + 1))
                if s >= MLP_AT and (s - MLP_AT) % 2 == 0 and (s - MLP_AT) // 2 < H1T + H2T:
                    k = (s - MLP_AT) // 2
                    if k == 0:
                        pe.wait_ge(mlp_in, 16 * 7)
                        pe.wait_ge(z_copied, 2 * (TILES - 1))
                    if k < H1T:
                        mlp1(0, k)
                    else:
                        mlp2(0, k - H1T)
            mlp3(0)
            layer2(TILES - 1, 0, F)
            pe.wait_ge(z_copied, 2 * TILES - 1)
            for k in range(3):
                mlp1(1, k, second=False)
            pe.wait_ge(z_copied, 2 * TILES)
            for k in range(3):
                mlp1(1, k, first=False)
            for k in range(3, H1T):
                mlp1(1, k)
            for k in range(H2T):
                mlp2(1, k)
            mlp3(1)


def _pairs():
    places = [(PT - 1) * len(range(n, P, F)) + (n < REST) for n in range(F)]
    owned = [{(n + k) % F for k in range((F + 1) // 2)} for n in range(F)]
    while True:
        over = [n for n in range(F) if len(owned[n]) > places[n]]
        if not over:
            break
        came, queue = {over[0]: None}, [over[0]]
        for n in queue:
            if len(owned[n]) < places[n]:
                break
            for m in sorted(owned[n]):
                if m not in came:
                    came[m] = n
                    queue.append(m)
        while came[n] is not None:
            owned[came[n]].remove(n)
            owned[n].add(came[n])
            n = came[n]
    pairs = np.full((PT, P, 2), -1)
    left = [sorted(o) for o in owned]
    for t in range(PT - 1):
        for p in range(P):
            pairs[t, p] = p % F, left[p % F].pop()
    for n in range(REST):
        m = left[n].pop()
        for at in REST_AT:
            pairs[PT - 1, at + n] = n, m
    assert not any(left)
    return pairs


def _selections(pairs):
    s = np.zeros((R, PT + 1, P), np.float32)
    for t in range(PT + 1):
        for p in range(P):
            m = pairs[t, p, 1] if t < PT else p % F
            if m >= 0:
                s[m::F, t, p] = 1.0
    return s


def kernel(**inputs):
    import concourse.bacc as bacc
    import ml_dtypes
    from concourse.bass_utils import run_bass_kernel_spmd

    a = {k: np.asarray(v) for k, v in inputs.items()}
    rows = [a[f"tbl_{f}"].shape[0] for f in range(F)]
    order = sorted(range(F), key=lambda f: rows[f])
    small = [f for f in order if rows[f] <= LOOK_MAX][:LOOK_N]
    blocks = sorted({rows[f] // LOOK_P for f in small})
    assert all(rows[f] % LOOK_P == 0 for f in small)
    pairs = _pairs()
    w0 = a["L0_rec_W0"]
    w0_pair = np.zeros((PT, P, O), w0.dtype)
    w0_mirror = np.zeros((PT, P, O), w0.dtype)
    for t, p in zip(*np.nonzero(pairs[:, :, 1] >= 0)):
        n, m = (order[x] for x in pairs[t, p])
        w0_pair[t, p] = w0[n * F + m]
        if n != m:
            w0_mirror[t, p] = w0[m * F + n]
    arrays = {
        "ids": np.ascontiguousarray(a["ids"].reshape(TILES, P, F).transpose(1, 0, 2)),
        "ids_small": np.ascontiguousarray(a["ids"][:P, small].T),
        "ids_again": np.ascontiguousarray(a["ids"][P:2 * P, small[:LOOK_AGAIN]].T),
        "row_numbers": np.concatenate([np.repeat(np.arange(LOOK_P * c).reshape(LOOK_P, c), P, axis=1) for c in blocks],
                                      axis=1).astype(np.int16),
        "dense_t": np.ascontiguousarray(a["dense_ctx"].T),
        "w0_pair": w0_pair,
        "w0_mirror": w0_mirror,
        "w1": a["L0_rec_W1"],
        "wt1": a["W_top1"],
        "bt1": np.ascontiguousarray(a["b_top1"].reshape(H1T, P).T),
        "wt2": a["W_top2"],
        "bt2": np.ascontiguousarray(a["b_top2"].reshape(H2T, P).T),
        "wt3": np.ascontiguousarray(a["W_top3"].reshape(H2T, P).T),
        "select": _selections(pairs).astype(ml_dtypes.bfloat16),
        "ident16": np.eye(P, dtype=ml_dtypes.bfloat16),
        "ident32": np.eye(P, dtype=np.float32),
    }
    arrays.update({f"tbl_{f}": a[f"tbl_{f}"] for f in range(F)})
    nc = bacc.Bacc("TRN2", target_bir_lowering=False, num_devices=1)
    aps = {k: nc.dram_tensor(k, v.shape, mybir.dt.from_np(v.dtype), kind="ExternalInput").ap()
           for k, v in arrays.items()}
    tables = [aps.pop(f"tbl_{f}") for f in range(F)]
    out = nc.dram_tensor("y", (B, 1), mybir.dt.float32, kind="ExternalOutput").ap()
    build(nc, tables=tables, order=order, out=out, **aps)
    return run_bass_kernel_spmd(nc, [arrays], core_ids=[0]).results[0]["y"]
```
